# Optimizing a Trainium2 kernel written in Bass

```python
import numpy as np
import jax
import jax.numpy as jnp

def _softmax(x, axis=-1):
    return jax.nn.softmax(x, axis=axis)
def _gelu(x):
    return jax.nn.gelu(x, approximate=True)
def _silu(x):
    return jax.nn.silu(x)
def _sigmoid(x):
    return jax.nn.sigmoid(x)
def _layernorm(x, axis=-1, eps=1e-5):
    m = jnp.mean(x, axis=axis, keepdims=True)
    v = jnp.var(x, axis=axis, keepdims=True)
    return (x - m) / jnp.sqrt(v + eps)
def _scatter_add(tgt, idx, src, axis=0):
    return tgt.at[idx].add(src)
def _segment_sum(src, seg, n):
    return jax.ops.segment_sum(src, seg, n)

kernel_name = 'mk_conv_preact_d1_conv_nchw64_6bfd1a'

def setup_inputs(seed: int = 0):
    np.random.seed(seed)
    _w = jnp.asarray
    def _rec_inputs():
        import jax
        import jax.numpy as jnp
        _gk = jax.random.key(seed)
        x = -0.000125 + 0.9999 * jax.random.normal(jax.random.fold_in(_gk, 1), (32, 64, 128, 128), jnp.float32)
        return x
    x = _rec_inputs()
    def _L0_conv_setup():
        import jax, jax.numpy as jnp
        import numpy as np
        B, CIN, COUT = (32, 64, 64)
        H = W = 128
        N_HEADS = 4
        MODES_X, MODES_Y = (64, 512)
        MPX = MODES_X // N_HEADS
        MPY = MODES_Y // N_HEADS
        WY = MPY // 2 + 1
        key = jax.random.key(seed)
        k1, k2, k3 = jax.random.split(key, 3)
        x = jax.random.normal(k1, (B, CIN, H, W), dtype=jnp.float32)
        weights_real = jax.random.normal(k2, (N_HEADS, CIN, COUT, MPX, WY), dtype=jnp.float32) * 0.01
        weights_imag = jax.random.normal(k3, (N_HEADS, CIN, COUT, MPX, WY), dtype=jnp.float32) * 0.01
        bias = jnp.zeros((COUT, 1, 1), dtype=jnp.float32)
        return {'x': x, 'weights_real': weights_real, 'weights_imag': weights_imag, 'bias': bias}
    _L0_conv_all = _L0_conv_setup()
    _L0_conv_in = {k: v for k, v in _L0_conv_all.items() if k in ('weights_real', 'weights_imag', 'bias', )}
    del _L0_conv_all

    return {
        "x": x,
        "L0_conv_weights_real": _L0_conv_in["weights_real"],
        "L0_conv_weights_imag": _L0_conv_in["weights_imag"],
        "L0_conv_bias": _L0_conv_in["bias"],
    }

def reference(x, L0_conv_weights_real, L0_conv_weights_imag, L0_conv_bias):
    import jax
    import jax.numpy as jnp
    def _L0_conv_ref(x, weights_real, weights_imag, bias):
        import jax, jax.numpy as jnp
        import numpy as np
        B, CIN, COUT = (32, 64, 64)
        H = W = 128
        N_HEADS = 4
        MODES_X, MODES_Y = (64, 512)
        MPX = MODES_X // N_HEADS
        MPY = MODES_Y // N_HEADS
        WY = MPY // 2 + 1
        Bn, C, Hn, Wn = x.shape
        n_heads, _, cout, mpx, wy = weights_real.shape
        x_freq = jnp.fft.rfft2(x, norm='ortho')
        freq_H, freq_W = (x_freq.shape[-2], x_freq.shape[-1])
        x_seg = x_freq[:, :, :n_heads * mpx, :].reshape(Bn, C, n_heads, mpx, freq_W)
        w = weights_real.astype(jnp.complex64) + 1j * weights_imag.astype(jnp.complex64)
        out_top = jnp.einsum('bihxy,hioxy->bohxy', x_seg, w)
        out_top = out_top.reshape(Bn, cout, n_heads * mpx, freq_W)
        out_freq = jnp.pad(out_top, ((0, 0), (0, 0), (0, freq_H - n_heads * mpx), (0, 0)))
        x_out = jnp.fft.irfft2(out_freq, s=(Hn, Wn), norm='ortho')
        return x_out + bias

    def _gn(v, G=32, eps=1e-5):
        B_, C_, H_, W_ = v.shape
        g = v.reshape(B_, G, C_ // G, H_, W_)
        m = jnp.mean(g, axis=(2, 3, 4), keepdims=True)
        s = jnp.var(g, axis=(2, 3, 4), keepdims=True)
        return ((g - m) / jnp.sqrt(s + eps)).reshape(v.shape)

    def _ln_c(v, eps=1e-6):
        m = jnp.mean(v, axis=1, keepdims=True)
        s = jnp.var(v, axis=1, keepdims=True)
        return (v - m) / jnp.sqrt(s + eps)

    def _ln_t(v, eps=1e-5):
        m = jnp.mean(v, axis=-1, keepdims=True)
        s = jnp.var(v, axis=-1, keepdims=True)
        return (v - m) / jnp.sqrt(s + eps)

    def _to_tokens(v):
        B_, C_, H_, W_ = v.shape
        return v.reshape(B_, C_, H_ * W_).transpose(0, 2, 1)
    def _from_tokens(t, like):
        B_, C_, H_, W_ = like.shape
        return t.transpose(0, 2, 1).reshape(B_, C_, H_, W_)

    x = x + _L0_conv_ref(_gn(x), L0_conv_weights_real, L0_conv_weights_imag, L0_conv_bias)
    return x


_drawn_inputs = setup_inputs


def setup_inputs(seed=0):
    import zlib

    import numpy as np

    out = dict(_drawn_inputs(seed))
    spreads = {'L0_conv_bias': (0.0, 0.1)}
    factors = {}
    for name, (base, spread) in spreads.items():
        noise = np.random.default_rng([zlib.crc32(name.encode()), seed]).standard_normal(out[name].shape)
        drawn = base * np.exp(spread * noise) if base else spread * noise
        out[name] = jnp.asarray(drawn.astype(out[name].dtype))
    for name, factor in factors.items():
        out[name] = (out[name] * factor).astype(out[name].dtype)
    return out
```

```python
import concourse.bass as bass
from concourse import mybir
from contextlib import ExitStack


def spectral_conv_kernel(nc, x, w_real, w_imag, bias, tables, out):
    fp32 = mybir.dt.float32
    ALU = mybir.AluOpType
    ACT = mybir.ActivationFunctionType

    B, C, H, W = x.shape
    HEADS, _, CO, MX, KY = w_real.shape
    KX = HEADS * MX
    KH = KY - 1
    P = 128
    EPS = 1e-5

    HB = B // 2
    UI = 2 * HB
    XS = 4
    CH = 8
    UC = UI // CH
    BODY1 = XS * UC
    ITER1 = (C // 2) * 2 // XS
    KG = 4
    NG = KX // KG
    NQ = KX // 2
    BODY2 = 4
    ITER2 = NQ // BODY2
    GK = 13
    GPQ = 2 * KY // GK
    XS3 = 4
    UC3 = B // CH
    BODY3 = XS3 * UC3
    ITER3 = CO // XS3

    ctx = ExitStack()
    with ctx:
        def sem(name):
            return ctx.enter_context(nc.semaphore(name))

        f_dram = nc.dram_tensor("f_spectrum", (NG, 2, C, KH, KG * B), fp32, kind="Internal").ap()
        f64_dram = nc.dram_tensor("f_nyquist", (2, KX, C, B), fp32, kind="Internal").ap()
        g_dram = nc.dram_tensor("g_spectrum", (KX, 2, CO, B * KY), fp32, kind="Internal").ap()

        NT = tables.shape[1] // P
        tab = ctx.enter_context(nc.sbuf_tensor("tab", [P, NT, P], fp32))
        dft_h, dft_wr, dft_wi, dft_z, inv_r, inv_i, inv_w = (tab[:, n, :] for n in range(NT))
        wring = ctx.enter_context(nc.sbuf_tensor("wring", [P, 2 * CO * 2 * KY], fp32))
        arena = ctx.enter_context(nc.sbuf_tensor("arena", [P, 3 * KY * KG * B + 2 * 2 * B * KY], fp32))
        bias_sb = ctx.enter_context(nc.sbuf_tensor("bias_sb", [P, CO], fp32))

        w_sb = wring[:, :].rearrange("p (s o m) -> p s o m", s=2, o=CO)
        used = 0

        def carve(n):
            nonlocal used
            used += n
            return arena[:, used - n:used]

        x1 = carve(XS * UI * W).rearrange("p (s c b w) -> p s c b w", s=XS, c=2, b=HB)
        t_sb = carve(2 * CH * P).rearrange("p (s r k b) -> p s r k b", s=2, r=2, k=KX)
        f_sb = carve(2 * 2 * KX * B).rearrange("p (s c k b) -> p s c k b", s=2, c=2, k=KX)
        st = carve(2 * UI * 6).rearrange("p (s c b v) -> p s c b v", s=2, c=2, b=HB)
        z_sb = carve(2 * 2 * B).rearrange("p (a c b) -> p a c b", a=2, c=2)
        zo_sb = carve(2 * 2 * B)
        msum2 = carve(2 * HB).rearrange("p (c b) -> p c b", c=2)
        msum = carve(HB)
        rows_sum = carve(HB)
        sums = carve(HB)
        neg_mean = carve(HB)
        dev = carve(2 * HB * 2).rearrange("p (c b v) -> p c b v", c=2, v=2)
        devsq = carve(2 * HB * 2).rearrange("p (c b v) -> p c b v", c=2, v=2)
        qsum2 = carve(2 * HB).rearrange("p (c b) -> p c b", c=2)
        qsum = carve(HB)
        consts = carve(6 * 4 * HB).rearrange("p (n m) -> p n m", n=6)
        zeros = carve(HB)
        fence = carve(1)
        var = carve(2 * HB).rearrange("p (s b) -> p s b", s=2)
        sd = carve(2 * HB).rearrange("p (s b) -> p s b", s=2)
        rs0 = carve(2 * HB).rearrange("p (s b) -> p s b", s=2)
        nt = carve(HB)
        nt2 = carve(HB)
        rstd = carve(2 * HB).rearrange("p (s b) -> p s b", s=2)
        nbias = carve(2 * HB).rearrange("p (s b) -> p s b", s=2)
        zdiff = carve(2 * HB).rearrange("p (c b) -> p c b", c=2)
        assert used <= arena.shape[1]
        used = 0
        planes = carve(3 * KY * KG * B).rearrange("p (s y k b) -> p s y k b", s=3, y=KY, k=KG)
        g_st = carve(2 * 2 * B * KY).rearrange("p (s n y) -> p s n y", s=2, n=2 * B)
        used = 0
        g3 = carve(XS3 * B * KY).rearrange("p (s b y) -> p s b y", s=XS3, b=B)
        v_sb = carve(2 * CH * H).rearrange("p (s b h) -> p s b h", s=2, b=CH)
        x3 = wring[:, 0:XS3 * B * W].rearrange("p (s b w) -> p s b w", s=XS3, b=B)

        ps = ctx.enter_context(nc.psum_tensor("ps", [P, 8, 512], fp32))
        ps_t = [ps[:, 2 * s:2 * s + 2, :].rearrange("p a (i r k) -> p (a i) r k", r=2, k=KX) for s in range(2)]
        ps_f = [ps[:, 4 + s, :] for s in range(2)]
        ps_z = ps[:, 6, 0:P]
        ps_g = [ps[:, 2 * s:2 * s + 2, :].rearrange("p a (y n) -> p (a y) n", n=2 * B) for s in range(4)]
        ps_v = [ps[:, 2 * s:2 * s + 2, :].rearrange("p a (i h) -> p (a i) h", h=H) for s in range(2)]
        ps_o = [ps[:, 4 + 2 * s:6 + 2 * s, :].rearrange("p a (i h) -> p (a i) h", h=H) for s in range(2)]

        tab_loaded = sem("tab_loaded")
        bias_loaded = sem("bias_loaded")
        x1_loaded = [sem(f"x1_loaded{s}") for s in range(XS)]
        consts_ready = sem("consts_ready")
        bn_done = sem("bn_done")
        pool_step = sem("pool_step")
        var_ready = sem("var_ready")
        sd_ready = sem("sd_ready")
        rs0_ready = sem("rs0_ready")
        scale_ready = sem("scale_ready")
        z_ready = sem("z_ready")
        norm_dve = sem("norm_dve")
        norm_act = sem("norm_act")
        t_done = sem("t_done")
        t_copied = sem("t_copied")
        f_done = sem("f_done")
        f_copied = sem("f_copied")
        z_done = sem("z_done")
        z_copied = sem("z_copied")
        f_stored = [sem(f"f_stored{s}") for s in range(2)]
        z_stored = sem("z_stored")
        w_loaded = [sem(f"w_loaded{s}") for s in range(2)]
        pl_loaded = [sem(f"pl_loaded{s}") for s in range(2)]
        pl_dve = sem("pl_dve")
        pl_act = sem("pl_act")
        mix_done = sem("mix_done")
        g_dve = sem("g_dve")
        g_act = sem("g_act")
        g_stored = [sem(f"g_stored{s}") for s in range(2)]
        x3_loaded = [sem(f"x3_loaded{s}") for s in range(XS3)]
        g3_loaded = [sem(f"g3_loaded{s}") for s in range(XS3)]
        v_done = sem("v_done")
        v_copied = sem("v_copied")
        o_done = sem("o_done")
        o_added = sem("o_added")
        stored = [sem(f"stored{s}") for s in range(XS3)]

        block = ctx.enter_context(nc.Block())

        def wait(e, s, value):
            if not isinstance(value, int) or value > 0:
                e.wait_ge(s, value)

        @block.sync
        def _(sp):
            def load_x1(i, j):
                for c in range(2):
                    for b in range(0, HB, CH):
                        b0 = HB * (j % 2) + b
                        src = x[b0:b0 + CH, bass.ds(i * 4 + (j // 2) * 2 + c, 1)].rearrange("b c h w -> h (b c) w")
                        sp.dma_start(x1[:, j, c, b:b + CH], src).then_inc(x1_loaded[j], 16)

            def store_f(i, a):
                sp.wait_ge(f_copied, i * BODY1 + (a + 1) * 2 * UC)
                for r in range(2):
                    for c in range(2):
                        dst = f_dram[:, r, bass.ds(i * 4 + a * 2 + c, 1)].rearrange("g c y m -> y (g c) m")
                        src = f_sb[KH * r:KH * r + KH, a, c].rearrange("p (g k) b -> p g (k b)", k=KG)
                        sp.dma_start(dst, src).then_inc(f_stored[a], 16)

            def store_z(i):
                sp.wait_ge(z_copied, i + 1)
                dst = f64_dram[:, :, bass.ds(i * 4, 4), :].rearrange("r k c b -> (r k) c b")
                sp.dma_start(dst, zo_sb.rearrange("p (c b) -> p c b", b=B)).then_inc(z_stored, 16)

            def load_w(t_head, x0, slot):
                for r, w in enumerate((w_real, w_imag)):
                    src = w.rearrange("h i o x y -> h i o (x y)")[bass.ds(t_head, 1), :, :, bass.ds(x0 * KY, 2 * KY)]
                    sp.dma_start(w_sb[C * r:C * r + C, slot], src.rearrange("h i o m -> (h i) o m"))\
                        .then_inc(w_loaded[slot], 16)

            for j in range(XS):
                load_x1(0, j)
                if j == 0:
                    sp.dma_start(tab[:, :, :].rearrange("p t n -> p (t n)"), tables).then_inc(tab_loaded, 16)
            sp.dma_start(bias_sb[:, :], bias.rearrange("c a b -> (a b) c").broadcast_to((P, CO))).then_inc(bias_loaded, 16)
            for q in range(2):
                load_w(0, 2 * q, q)
            with sp.Fori(0, ITER1 - 1) as i:
                for j in range(XS):
                    sp.wait_ge(t_done, i * BODY1 + (j + 1) * UC)
                    load_x1(i + 1, j)
                    if j % 2:
                        store_f(i, j // 2)
                store_z(i)
            for a in range(2):
                store_f(ITER1 - 1, a)
            store_z(ITER1 - 1)
            for a in range(2):
                sp.wait_ge(f_stored[a], 64 * ITER1)
            sp.wait_ge(z_stored, 16 * ITER1)

            def rows(t, i, j, lo, hi):
                return t[lo:hi, bass.ds(i * XS3 + j, 1)].rearrange("b c h w -> h (b c) w")

            def load_x3(i, j):
                for b in range(0, B, CH):
                    sp.dma_start(x3[:, j, b:b + CH], rows(x, i, j, b, b + CH)).then_inc(x3_loaded[j], 16)

            def load_planes(g, s):
                dst = planes[:, 2 * s]
                for r in range(2):
                    half = dst[C * (r ^ s):C * (r ^ s) + C]
                    src = f_dram[bass.ds(g, 1), r].rearrange("g c y m -> (g c) (y m)")
                    sp.dma_start(half[:, 0:KH].rearrange("p y k b -> p (y k b)"), src).then_inc(pl_loaded[s], 16)
                    src = f64_dram[r, bass.ds(g * KG, KG)].rearrange("k c b -> c k b")
                    sp.dma_start(half[:, KH], src).then_inc(pl_loaded[s], 16)

            def store_g(i, m):
                sp.wait_ge(g_dve, (i * BODY2 + m + 1) * (GPQ // 2))
                sp.wait_ge(g_act, (i * BODY2 + m + 1) * (GPQ // 2))
                for k in range(2):
                    dst = g_dram[bass.ds((i * BODY2 + m) * 2 + k, 1)].rearrange("k r o m -> (k o) r m")
                    src = g_st[CO * k:CO * k + CO, m % 2].rearrange("p (r b) y -> p r (b y)", r=2)
                    sp.dma_start(dst, src).then_inc(g_stored[m % 2], 16)

            load_planes(0, 0)
            load_planes(1, 1)

            def mix_turn(i, m, head, x0, last):
                sp.wait_ge(mix_done, (i * BODY2 + m + 1) * GPQ)
                if not (last and m >= BODY2 - 2):
                    load_w(head, x0, m % 2)
                elif m == BODY2 - 2:
                    load_x3(0, 0)
                    load_x3(0, 1)
                if m % 2 and not last:
                    load_planes(i * 2 + 2 + m // 2, m // 2)
                store_g(i, m)

            def mix_body(i, head, half, last=False):
                for m in range(BODY2):
                    at = m + 2
                    if at < BODY2:
                        mix_turn(i, m, head, half * 2 * BODY2 + 2 * at, last)
                    elif half == 0:
                        mix_turn(i, m, head, 2 * BODY2 + 2 * (at - BODY2), last)
                    else:
                        mix_turn(i, m, head + 1, 2 * (at - BODY2), last)

            mix_body(0, 0, 0)
            mix_body(1, 0, 1)
            with sp.Fori(1, HEADS - 1) as hd:
                mix_body(hd * 2, hd, 0)
                mix_body(hd * 2 + 1, hd, 1)
            mix_body(ITER2 - 2, HEADS - 1, 0)
            mix_body(ITER2 - 1, HEADS - 1, 1, last=True)

            def load_g3(i, j):
                src = g_dram.rearrange("k r o m -> (k r) o m")[:, bass.ds(i * XS3 + j, 1)]
                sp.dma_start(g3[:, j].rearrange("p b y -> p (b y)"), src.rearrange("p o m -> p (o m)"))\
                    .then_inc(g3_loaded[j], 16)

            def store_out(i, j):
                sp.wait_ge(o_added, i * BODY3 + (j + 1) * UC3)
                sp.dma_start(rows(out, i, j, 0, B), x3[:, j]).then_inc(stored[j], 16)

            for s in range(2):
                sp.wait_ge(g_stored[s], 32 * (NQ // 2))
            for j in range(XS3):
                load_g3(0, j)
                if j % 2:
                    load_x3(0, 1 + (j + 1) // 2)

            with sp.Fori(0, ITER3 - 1) as i:
                for j in range(XS3):
                    sp.wait_ge(v_done, i * BODY3 + (j + 1) * UC3)
                    load_g3(i + 1, j)
                    store_out(i, j)
                    if j > 0:
                        sp.wait_ge(stored[j - 1], (i + 1) * 16)
                        load_x3(i + 1, j - 1)
                sp.wait_ge(stored[XS3 - 1], (i + 1) * 16)
                load_x3(i + 1, XS3 - 1)
            for j in range(XS3):
                store_out(ITER3 - 1, j)
            for j in range(XS3):
                sp.wait_ge(stored[j], 16 * ITER3)

        STEPS = 20
        NEG_MEAN, SEG, VAR, EPSILON, HALF, THREE_HALVES = range(6)

        @block.gpsimd
        def _(pool):
            for n, value in enumerate((-1.0 / (4 * P), float(W // 2), 1.0 / (2 * H * W), EPS, -0.5, 1.5)):
                ins = nc.gpsimd.memset(consts[:, n], value)
            nc.gpsimd.memset(zeros[:, :], 0.0)
            ins = nc.gpsimd.memset(fence[:, :], 0.0)
            ins.then_inc(consts_ready, 1)
            pool.wait_ge(consts_ready, 1)

            def unit(i, j, first):
                s = j % 2
                u = i * XS + j
                steps = [0]

                def then(ins):
                    steps[0] += 1
                    ins.then_inc(pool_step, 1)
                    pool.wait_ge(pool_step, u * STEPS + steps[0])

                def tt(o, a, b, op):
                    return nc.gpsimd.tensor_tensor(o, a, b, op)

                def sum_over_rows(o, a):
                    then(tt(rows_sum[:, :], a, zeros[:, :], ALU.add))
                    nc.gpsimd.tensor_tensor(fence[:, :], zeros[:, 0:1], zeros[:, 0:1], ALU.add)
                    then(nc.gpsimd.partition_all_reduce(o, rows_sum[:, :], P, bass.bass_isa.ReduceOp.add))

                def const(n):
                    return consts[:, n, 0:HB]

                me_mo = st[:, s].rearrange("p c b (e v) -> p c b e v", e=2)[:, :, :, :, 1]
                m2 = st[:, s].rearrange("p c b (e v) -> p c b e v", e=2)[:, :, :, :, 2]
                pool.wait_ge(bn_done, u + 1)
                then(tt(msum2[:, :, :], me_mo[:, :, :, 0], me_mo[:, :, :, 1], ALU.add))
                then(tt(msum[:, :], msum2[:, 0], msum2[:, 1], ALU.add))
                sum_over_rows(sums[:, :], msum[:, :])
                then(tt(neg_mean[:, :], sums[:, :], const(NEG_MEAN), ALU.mult))
                for e in range(2):
                    for c in range(2):
                        ins = tt(dev[:, c, :, e], me_mo[:, c, :, e], neg_mean[:, :], ALU.add)
                then(ins)
                then(tt(devsq[:, :, :, :], dev[:, :, :, :], dev[:, :, :, :], ALU.mult))
                then(tt(dev[:, :, :, :], devsq[:, :, :, :],
                        consts[:, SEG].rearrange("p (c b v) -> p c b v", c=2, v=2), ALU.mult))
                then(tt(devsq[:, :, :, :], dev[:, :, :, :], m2, ALU.add))
                then(tt(qsum2[:, :, :], devsq[:, :, :, 0], devsq[:, :, :, 1], ALU.add))
                then(tt(qsum[:, :], qsum2[:, 0], qsum2[:, 1], ALU.add))
                sum_over_rows(sums[:, :], qsum[:, :])
                then(tt(nt[:, :], sums[:, :], const(VAR), ALU.mult))
                tt(var[:, s], nt[:, :], const(EPSILON), ALU.add).then_inc(var_ready, 1)
                pool.wait_ge(var_ready, u + 1)
                pool.wait_ge(rs0_ready, u + 1)
                then(tt(nt[:, :], rs0[:, s], rs0[:, s], ALU.mult))
                then(tt(nt2[:, :], nt[:, :], var[:, s], ALU.mult))
                then(tt(nt[:, :], nt2[:, :], const(HALF), ALU.mult))
                then(tt(nt2[:, :], nt[:, :], const(THREE_HALVES), ALU.add))
                wait(pool, norm_dve, u - 1)
                wait(pool, norm_act, u - 1)
                then(tt(rstd[:, s], nt2[:, :], rs0[:, s], ALU.mult))
                tt(nbias[:, s], neg_mean[:, :], rstd[:, s], ALU.mult).then_inc(scale_ready, 1)
                then(tt(zdiff[:, :, :], me_mo[:, :, :, 0], me_mo[:, :, :, 1], ALU.subtract))
                if j == 0:
                    wait(pool, z_done, i)
                for c in range(2):
                    ins = tt(z_sb[:, j // 2, c, HB * (j % 2):HB * (j % 2) + HB], zdiff[:, c], rstd[:, s], ALU.mult)
                ins.then_inc(z_ready, 1)
                assert steps[0] == STEPS, steps

            for j in range(XS):
                unit(0, j, True)
            with pool.Fori(1, ITER1) as i:
                for j in range(XS):
                    unit(i, j, False)

        ND = HB // 2

        @block.vector
        def _(dve):
            def stats(i, j):
                dve.wait_ge(x1_loaded[j], (i + 1) * 16 * UC)
                wait(dve, z_ready, i * XS + j - 1)
                for n in range(UI):
                    ins = nc.vector.bn_stats(st[:, j % 2, n // HB, n % HB], x1[:, j, n // HB, n % HB])
                ins.then_inc(bn_done, 1)

            def reciprocal(i, j):
                dve.wait_ge(sd_ready, i * XS + j + 1)
                nc.vector.reciprocal(rs0[:, j % 2], sd[:, j % 2]).then_inc(rs0_ready, 1)

            def normalise(i, j):
                dve.wait_ge(scale_ready, i * XS + j + 1)
                for b in range(ND):
                    v = x1[:, j, :, b]
                    ins = nc.vector.tensor_scalar(v, v, rstd[:, j % 2, b:b + 1], nbias[:, j % 2, b:b + 1],
                                                  ALU.mult, ALU.add)
                ins.then_inc(norm_dve, 1)

            def turn(i, j, last):
                reciprocal(i, j)
                if not last:
                    stats(*((i, j + 1) if j + 1 < XS else (i + 1, 0)))
                normalise(i, j)

            stats(0, 0)
            for j in range(XS):
                turn(0, j, False)
            with dve.Fori(1, ITER1 - 1) as i:
                for j in range(XS):
                    turn(i, j, False)
            for j in range(XS):
                turn(ITER1 - 1, j, j == XS - 1)

            def build(i, m):
                s, k = m // 2, 2 * (m % 2)
                if m % 2 == 0:
                    dve.wait_ge(pl_loaded[s], (i + 1) * 64)
                wait(dve, mix_done, (i * BODY2 + m - 1) * GPQ)
                a = planes[0:C, 1, :, k:k + 2]
                b = planes[C:P, 2 * s, :, k:k + 2]
                ins = nc.vector.tensor_copy(a, b)
                if s == 0:
                    ins = nc.vector.tensor_scalar(b, b, -1.0, None, ALU.mult)
                ins.then_inc(pl_dve, 1)

            def copy_groups(i, m):
                wait(dve, g_stored[m % 2], i * 64 + (m // 2) * 32)
                for n in range(0, GPQ, 2):
                    k, y = n // (GPQ // 2), n % (GPQ // 2) * GK
                    dve.wait_ge(mix_done, (i * BODY2 + m) * GPQ + n + 1)
                    src = ps_g[(m * GPQ + n) % 4][C * k:C * k + C, 0:GK]
                    dst = g_st[C * k:C * k + C, m % 2, :, y:y + GK].rearrange("p n y -> p y n")
                    nc.vector.tensor_copy(dst, src).then_inc(g_dve, 1)

            def mix_turn(i, m, last=False):
                if not last:
                    build(*((i, m + 1) if m + 1 < BODY2 else (i + 1, 0)))
                copy_groups(i, m)

            build(0, 0)
            for m in range(BODY2):
                mix_turn(0, m)
            with dve.Fori(1, ITER2 - 1) as i:
                for m in range(BODY2):
                    mix_turn(i, m)
            for m in range(BODY2):
                mix_turn(ITER2 - 1, m, m == BODY2 - 1)

            def add_x(i, n):
                j, b0 = n // UC3, n % UC3 * CH
                if n % UC3 == 0:
                    dve.wait_ge(x3_loaded[j], (i + 1) * 16 * UC3)
                dve.wait_ge(o_done, i * BODY3 + n + 1)
                v = x3[:, j, b0:b0 + CH]
                nc.vector.scalar_tensor_tensor(out=v, in0=ps_o[n % 2], scalar=bias_sb[:, bass.ds(i * XS3 + j, 1)],
                                               in1=v, op0=ALU.add, op1=ALU.add).then_inc(o_added, 1)

            dve.wait_ge(bias_loaded, 16)

            with dve.Fori(0, ITER3) as i:
                for n in range(BODY3):
                    add_x(i, n)

        @block.scalar
        def _(act):
            def root(i, j):
                act.wait_ge(var_ready, i * XS + j + 1)
                nc.scalar.activation(sd[:, j % 2], var[:, j % 2], ACT.Sqrt).then_inc(sd_ready, 1)

            def normalise(i, j, lo, hi):
                if lo == ND:
                    act.wait_ge(scale_ready, i * XS + j + 1)
                for b in range(lo, hi):
                    v = x1[:, j, :, b]
                    ins = nc.scalar.activation(v, v, ACT.Identity, bias=nbias[:, j % 2, b:b + 1],
                                               scale=rstd[:, j % 2, b:b + 1])
                if hi == HB:
                    ins.then_inc(norm_act, 1)

            def copy_t(i, m):
                act.wait_ge(t_done, i * BODY1 + m + 1)
                wait(act, f_done, i * BODY1 + m - 1)
                dst = t_sb[:, m % 2].rearrange("p r k b -> p b r k")
                nc.scalar.activation(dst, ps_t[m % 2], ACT.Copy).then_inc(t_copied, 1)

            def copy_f(i, m):
                a = m // (2 * UC)
                if m % (2 * UC) == 0:
                    wait(act, f_stored[a], i * 64)
                act.wait_ge(f_done, i * BODY1 + m + 1)
                c = m % UC // (UC // 2)
                b0 = (m // UC % 2) * HB + m % (UC // 2) * CH
                src = ps_f[m % 2].rearrange("p (k b) -> p k b", b=CH)
                nc.scalar.activation(f_sb[:, a, c, :, b0:b0 + CH], src, ACT.Copy).then_inc(f_copied, 1)

            def copy_z(i):
                act.wait_ge(z_done, i + 1)
                wait(act, z_stored, i * 16)
                nc.scalar.activation(zo_sb, ps_z, ACT.Copy).then_inc(z_copied, 1)

            NORM = [ND, ND + 2, ND + 5, HB, HB]

            def after(i, j, n):
                return (i, j + n) if j + n < XS else (i + 1, j + n - XS)

            def turn(i, j, first=False, left=XS):
                for n in range(UC):
                    m = j * UC + n
                    copy_t(i, m)
                    if left > 1 and NORM[n + 1] > NORM[n]:
                        normalise(*after(i, j, 1), NORM[n], NORM[n + 1])
                    if left > 2 and n == UC - 1:
                        root(*after(i, j, 2))
                    if m:
                        copy_f(i, m - 1)
                    elif not first:
                        copy_f(i - 1, BODY1 - 1)
                        copy_z(i - 1)

            root(0, 0)
            normalise(0, 0, ND, HB)
            root(0, 1)
            for j in range(XS):
                turn(0, j, first=True)
            with act.Fori(1, ITER1 - 1) as i:
                for j in range(XS):
                    turn(i, j)
            for j in range(XS):
                turn(ITER1 - 1, j, left=XS - j)
            copy_f(ITER1 - 1, BODY1 - 1)
            copy_z(ITER1 - 1)

            def build(i, m):
                s, k = m // 2, 2 * (m % 2)
                if m % 2 == 0:
                    act.wait_ge(pl_loaded[s], (i + 1) * 64)
                wait(act, mix_done, (i * BODY2 + m - 1) * GPQ)
                nc.scalar.activation(planes[C:P, 1, :, k:k + 2], planes[0:C, 2 * s, :, k:k + 2], ACT.Copy,
                                     scale=-1.0 if s else 1.0).then_inc(pl_act, 1)

            def copy_groups(i, m):
                wait(act, g_stored[m % 2], i * 64 + (m // 2) * 32)
                for n in range(1, GPQ, 2):
                    k, y = n // (GPQ // 2), n % (GPQ // 2) * GK
                    act.wait_ge(mix_done, (i * BODY2 + m) * GPQ + n + 1)
                    src = ps_g[(m * GPQ + n) % 4][C * k:C * k + C, 0:GK]
                    dst = g_st[C * k:C * k + C, m % 2, :, y:y + GK].rearrange("p n y -> p y n")
                    nc.scalar.activation(dst, src, ACT.Copy).then_inc(g_act, 1)

            def mix_turn(i, m, last=False):
                if not last:
                    build(*((i, m + 1) if m + 1 < BODY2 else (i + 1, 0)))
                copy_groups(i, m)

            build(0, 0)
            for m in range(BODY2):
                mix_turn(0, m)
            with act.Fori(1, ITER2 - 1) as i:
                for m in range(BODY2):
                    mix_turn(i, m)
            for m in range(BODY2):
                mix_turn(ITER2 - 1, m, m == BODY2 - 1)

            def copy_v(i, n):
                act.wait_ge(v_done, i * BODY3 + n + 1)
                wait(act, o_done, i * BODY3 + n - 1)
                nc.scalar.activation(v_sb[:, n % 2], ps_v[n % 2], ACT.Copy).then_inc(v_copied, 1)

            for n in range(BODY3):
                copy_v(0, n)
            with act.Fori(1, ITER3) as i:
                for n in range(BODY3):
                    copy_v(i, n)

        @block.tensor
        def _(pe):
            def dft_rows(i, m):
                j, n = m // UC, m % UC
                if n == 0:
                    pe.wait_ge(norm_dve, i * XS + j + 1)
                    pe.wait_ge(norm_act, i * XS + j + 1)
                wait(pe, t_copied, i * BODY1 + m - 1)
                c, b0 = n // (UC // 2), n % (UC // 2) * CH
                for b in range(CH):
                    ins = nc.tensor.matmul(ps_t[m % 2][:, b].rearrange("p r k -> p (r k)"), x1[:, j, c, b0 + b],
                                           dft_h, start=True, stop=True)
                ins.then_inc(t_done, 1)

            def dft_cols(i, m):
                pe.wait_ge(t_copied, i * BODY1 + m + 1)
                wait(pe, f_copied, i * BODY1 + m - 1)
                nc.tensor.matmul(ps_f[m % 2], dft_wr, t_sb[:, m % 2, 0].rearrange("p k b -> p (k b)"),
                                 start=True, stop=False)
                nc.tensor.matmul(ps_f[m % 2], dft_wi, t_sb[:, m % 2, 1].rearrange("p k b -> p (k b)"),
                                 start=False, stop=True).then_inc(f_done, 1)

            def dft_nyquist(i):
                pe.wait_ge(z_ready, (i + 1) * XS)
                wait(pe, z_copied, i)
                nc.tensor.matmul(ps_z, dft_z, z_sb[:, :, :, :].rearrange("p a c b -> p (a c b)"),
                                 start=True, stop=True).then_inc(z_done, 1)

            def body(i, first):
                for m in range(BODY1):
                    if m == (XS - 1) * UC + 1:
                        dft_nyquist(i)
                    dft_rows(i, m)
                    if m:
                        dft_cols(i, m - 1)
                    elif not first:
                        dft_cols(i - 1, BODY1 - 1)

            pe.wait_ge(tab_loaded, 16)
            body(0, True)
            with pe.Fori(1, ITER1) as i:
                body(i, False)
            dft_cols(ITER1 - 1, BODY1 - 1)

            pe.wait_ge(f_copied, ITER1 * BODY1)
            pe.wait_ge(z_copied, ITER1)

            def mix_pair(i, m):
                s = m // 2
                pe.wait_ge(w_loaded[m % 2], i * 64 + (m // 2 + 1) * 32)
                pe.wait_ge(pl_dve, i * BODY2 + m + 1)
                pe.wait_ge(pl_act, i * BODY2 + m + 1)
                for n in range(GPQ):
                    seen = (m * GPQ + n) // 2 - 1
                    wait(pe, g_dve if n % 2 == 0 else g_act, i * (BODY2 * GPQ // 2) + seen)
                    k, y0 = n // (GPQ // 2), n % (GPQ // 2) * GK
                    for y in range(GK):
                        ins = nc.tensor.matmul(ps_g[(m * GPQ + n) % 4][C * k:C * k + C, y],
                                               w_sb[:, m % 2, :, k * KY + y0 + y],
                                               planes[:, s:s + 2, y0 + y, 2 * (m % 2) + k, :],
                                               start=True, stop=True)
                    ins.then_inc(mix_done, 1)

            for m in range(BODY2):
                mix_pair(0, m)
            with pe.Fori(1, ITER2) as i:
                for m in range(BODY2):
                    mix_pair(i, m)

            pe.wait_ge(g_dve, NQ * GPQ // 2)
            pe.wait_ge(g_act, NQ * GPQ // 2)

            def inverse_rows(i, n):
                j, b0 = n // UC3, n % UC3 * CH
                if n % UC3 == 0:
                    pe.wait_ge(g3_loaded[j], i * 16 + 16)
                wait(pe, v_copied, i * BODY3 + n - 1)
                for c in range(CH):
                    for r, t in enumerate((inv_r, inv_i)):
                        ins = nc.tensor.matmul(ps_v[n % 2][KH * r:KH * r + KH, c], g3[:, j, b0 + c, r:r + KH], t,
                                               start=True, stop=True)
                ins.then_inc(v_done, 1)

            def inverse_cols(i, n):
                pe.wait_ge(v_copied, i * BODY3 + n + 1)
                wait(pe, o_added, i * BODY3 + n - 1)
                for c in range(CH):
                    ins = nc.tensor.matmul(ps_o[n % 2][:, c], v_sb[:, n % 2, c], inv_w, start=True, stop=True)
                ins.then_inc(o_done, 1)

            def inverse_body(i, first):
                for n in range(BODY3):
                    inverse_rows(i, n)
                    if n:
                        inverse_cols(i, n - 1)
                    elif not first:
                        inverse_cols(i - 1, BODY3 - 1)

            inverse_body(0, True)
            with pe.Fori(1, ITER3) as i:
                inverse_body(i, False)
            inverse_cols(ITER3 - 1, BODY3 - 1)


def dft_tables(n, kx, ky):
    import numpy as np

    a = 2 * np.pi / n
    p = np.arange(n)[:, None]
    k = np.arange(kx)[None, :]
    c, s = np.cos(a * p * k), np.sin(a * p * k)
    dft_h = np.concatenate([c, -s], 1) / n
    dft_wr = np.concatenate([c, -s], 1)
    dft_wi = np.concatenate([s, c], 1)
    dft_z = np.concatenate([s, c], 1) / n * (n // 2)
    h = np.arange(n)[None, :]
    kk = np.arange(kx)[:, None]
    c, s = np.cos(a * kk * h), np.sin(a * kk * h)
    inv_r = np.stack([c, -s], 1).reshape(2 * kx, n)
    inv_i = np.stack([s, c], 1).reshape(2 * kx, n)
    y = np.arange(ky)[:, None]
    cy, sy = np.cos(a * y * h), np.sin(a * y * h)
    weight = np.where((y == 0) | (y == ky - 1), 1.0, 2.0) / n
    inv_w = np.concatenate([(weight * cy)[:ky - 1], (-weight * sy)[1:ky - 1], (weight * cy)[ky - 1:]], 0)
    return np.ascontiguousarray(np.concatenate([dft_h, dft_wr, dft_wi, dft_z, inv_r, inv_i, inv_w], 1), np.float32)


_INS = ["x", "L0_conv_weights_real", "L0_conv_weights_imag", "L0_conv_bias"]


def kernel(**inputs):
    import numpy as _np
    import concourse.bacc as _bacc
    from concourse import mybir as _mybir
    from concourse.bass_utils import run_bass_kernel_spmd as _run

    nc = _bacc.Bacc("TRN2", target_bir_lowering=False, num_devices=1)
    arrays, args = {}, []
    for name in _INS:
        arrays[f"in_{name}_dram"] = _np.ascontiguousarray(inputs[name])
    n = inputs["x"].shape[-1]
    arrays["in_tables_dram"] = dft_tables(n, n // 2, n // 2 + 1)
    for name, a in arrays.items():
        args.append(nc.dram_tensor(name, a.shape, _mybir.dt.from_np(a.dtype), kind="ExternalInput").ap())
    shape = tuple(inputs["x"].shape)
    args.append(nc.dram_tensor("out_0_dram", shape, _mybir.dt.float32, kind="ExternalOutput").ap())
    spectral_conv_kernel(nc, *args)
    r = _run(nc, [arrays], core_ids=[0])
    return r.results[0]["out_0_dram"]
```

```python
import concourse.bass as bass
from concourse import mybir
from contextlib import ExitStack


def spectral_conv_kernel(nc, x, w_real, w_imag, bias, tables, out):
    fp32 = mybir.dt.float32
    fp16 = mybir.dt.float16
    ALU = mybir.AluOpType
    ACT = mybir.ActivationFunctionType

    B, C, H, W = x.shape
    HEADS, _, CO, MX, KY = w_real.shape
    KX = HEADS * MX
    KH = KY - 1
    P = 128
    EPS = 1e-5

    XS = 4
    CH = 8
    TH = CH // 2
    UC = 2 * B // CH
    BODY1 = XS * UC
    ITER1 = C // 2 // XS
    TS = 4
    NA = 12
    FIRST_A, FIRST_D = 9, 24
    LEAD = 5 * CH
    T_SCALE = 2048.0
    W_SCALE = 256.0
    KG = 4
    NG = KX // KG
    NQ = KX // 2
    BODY2 = 4
    ITER2 = NQ // BODY2
    GK = 13
    GPQ = 2 * KY // GK
    WP = 4
    XS3 = 4
    UC3 = B // CH
    BODY3 = XS3 * UC3
    ITER3 = CO // XS3
    V_TOP = 32768.0
    V_PER_W = float(C * H * W) ** 0.5 * float(2 * C * KX) ** 0.5
    V_PER_BIAS = float(W)
    TINY = 1e-30

    ctx = ExitStack()
    with ctx:
        def sem(name):
            return ctx.enter_context(nc.semaphore(name))

        f_dram = nc.dram_tensor("f_spectrum", (NG, 2, C, KH, KG * B), fp32, kind="Internal").ap()
        f64_dram = nc.dram_tensor("f_nyquist", (2, KX, C, B), fp32, kind="Internal").ap()
        g_dram = nc.dram_tensor("g_spectrum", (KX, 2, CO, B * KY), fp32, kind="Internal").ap()

        NT = tables.shape[1] // P
        tab = ctx.enter_context(nc.sbuf_tensor("tab", [P, NT, P], fp32))
        dft_h, dft_wr, dft_wi, dft_z, inv_r, inv_i, inv_w = (tab[:, n, :] for n in range(NT))
        dft_w16 = ctx.enter_context(nc.sbuf_tensor("dft_w16", [P, 2, 2, P], fp16))
        wring = ctx.enter_context(nc.sbuf_tensor("wring", [P, 2 * CO * 2 * KY], fp32))
        arena = ctx.enter_context(nc.sbuf_tensor("arena", [P, 3 * KY * KG * B + 2 * 2 * B * KY], fp32))
        inv_w16 = ctx.enter_context(nc.sbuf_tensor("inv_w16", [P, 2, P], fp16))
        small = ctx.enter_context(nc.sbuf_tensor("small", [P, 2 * BODY2 * WP + 10], fp32))
        w_max, w_run = small[:, 0:BODY2 * WP], small[:, BODY2 * WP:2 * BODY2 * WP]
        own_max, all_max, bias_col, bias_w, bound, bound_rec, v_scale, v_unscale = (
            small[:, 2 * BODY2 * WP + a:2 * BODY2 * WP + b]
            for a, b in ((0, 2), (2, 4), (4, 5), (5, 6), (6, 7), (7, 8), (8, 9), (9, 10)))

        w_sb = wring[:, :].rearrange("p (s o m) -> p s o m", s=2, o=CO)
        used = 0

        def carve(n):
            nonlocal used
            used += n
            return arena[:, used - n:used]

        def pairs(t):
            return t.rearrange("p (c b) -> p c b", c=2)

        half = 2 * B * W
        x1 = [t.rearrange("p (c b w) -> p c b w", c=2, b=B)
              for t in (carve(half), carve(half), wring[:, 0:half], wring[:, wring.shape[1] - half:])]
        t16 = carve(TS * CH * P).bitcast(fp16).rearrange("p (s v r k b) -> p s v r k b", s=TS, v=2, r=2, k=KX)
        f_sb = carve(2 * 2 * KX * B).rearrange("p (s c k b) -> p s c k b", s=2, c=2, k=KX)
        st = carve(2 * 2 * B * 6).rearrange("p (s c b v) -> p s c b v", s=2, c=2, b=B)
        z_sb = carve(XS * 2 * B).rearrange("p (a c b) -> p a c b", a=XS, c=2)
        zo_sb = carve(XS * 2 * B)
        msum2, qsum2, zdiff = pairs(carve(2 * B)), pairs(carve(2 * B)), pairs(carve(2 * B))
        dev = carve(4 * B).rearrange("p (c b v) -> p c b v", c=2, v=2)
        devsq = carve(4 * B).rearrange("p (c b v) -> p c b v", c=2, v=2)
        msum, qsum, sums, neg_mean, var_n, nt, nt2 = (carve(B) for _ in range(7))
        var, sd, rs0, rstd, nbias = (pairs(carve(2 * B)) for _ in range(5))
        seg_const = carve(4 * B).rearrange("p (c b v) -> p c b v", c=2, v=2)
        consts = carve(5 * B).rearrange("p (n m) -> p n m", n=5)
        fence = carve(2)
        assert used <= arena.shape[1]
        used = 0
        planes = carve(3 * KY * KG * B).rearrange("p (s y k b) -> p s y k b", s=3, y=KY, k=KG)
        g_st = carve(2 * 2 * B * KY).rearrange("p (s n y) -> p s n y", s=2, n=2 * B)
        used = 0
        g3 = carve(XS3 * B * KY).rearrange("p (s b y) -> p s b y", s=XS3, b=B)
        v16 = carve(2 * CH * H).bitcast(fp16).rearrange("p (s v b h) -> p s v b h", s=2, v=2, b=CH)
        x3 = wring[:, 0:XS3 * B * W].rearrange("p (s b w) -> p s b w", s=XS3, b=B)

        ps = ctx.enter_context(nc.psum_tensor("ps", [P, 8, 512], fp32))
        ps_t = [ps[:, s, :].rearrange("p (i r k) -> p i r k", r=2, k=KX) for s in range(TS)]
        ps_f = [ps[:, TS + s, :] for s in range(2)]
        ps_z = ps[:, TS + 2, 0:XS * 2 * B]
        ps_g = [ps[:, 2 * s:2 * s + 2, :].rearrange("p a (y n) -> p (a y) n", n=2 * B) for s in range(4)]
        ps_v = [ps[:, 2 * s:2 * s + 2, :].rearrange("p a (i h) -> p (a i) h", h=H) for s in range(2)]
        ps_o = [ps[:, 4 + 2 * s:6 + 2 * s, :].rearrange("p a (i h) -> p (a i) h", h=H) for s in range(2)]

        tab_loaded = sem("tab_loaded")
        bias_zeroed = sem("bias_zeroed")
        bias_loaded = sem("bias_loaded")
        bias_ready = sem("bias_ready")
        first_loaded = [sem(f"first_loaded{n}") for n in range(UC)]
        x1_loaded = [sem(f"x1_loaded{s}") for s in range(XS)]
        consts_ready = sem("consts_ready")
        bn_done = sem("bn_done")
        pool_step = sem("pool_step")
        var_ready = sem("var_ready")
        sd_ready = sem("sd_ready")
        rs0_ready = sem("rs0_ready")
        scale_ready = sem("scale_ready")
        zdiff_ready = sem("zdiff_ready")
        z_ready = sem("z_ready")
        split_ready = sem("split_ready")
        norm_first = sem("norm_first")
        norm_pool = sem("norm_pool")
        norm_act = sem("norm_act")
        t_done = sem("t_done")
        t_high = sem("t_high")
        t_low = sem("t_low")
        f_done = sem("f_done")
        f_copied = sem("f_copied")
        z_done = sem("z_done")
        z_copied = sem("z_copied")
        f_stored = [sem(f"f_stored{s}") for s in range(2)]
        z_stored = sem("z_stored")
        w_loaded = [sem(f"w_loaded{s}") for s in range(2)]
        pl_loaded = [sem(f"pl_loaded{s}") for s in range(2)]
        pl_dve = sem("pl_dve")
        pl_act = sem("pl_act")
        mix_done = sem("mix_done")
        w_seen = sem("w_seen")
        w_run_ready = sem("w_run_ready")
        own_max_ready = sem("own_max_ready")
        all_max_ready = sem("all_max_ready")
        scale_step = sem("scale_step")
        bias_added = sem("bias_added")
        g_dve = sem("g_dve")
        g_act = sem("g_act")
        g_stored = [sem(f"g_stored{s}") for s in range(2)]
        x3_loaded = [sem(f"x3_loaded{s}") for s in range(XS3)]
        g3_loaded = [sem(f"g3_loaded{s}") for s in range(XS3)]
        v_done = sem("v_done")
        v_high = sem("v_high")
        v_low = sem("v_low")
        o_done = sem("o_done")
        o_added = sem("o_added")
        stored = [sem(f"stored{s}") for s in range(XS3)]

        block = ctx.enter_context(nc.Block())

        def wait(e, s, value):
            if not isinstance(value, int) or value > 0:
                e.wait_ge(s, value)

        @block.sync
        def _(sp):
            def load_x1(i, j):
                for c in range(2):
                    for b in range(0, B, CH):
                        src = x[b:b + CH, bass.ds((i * XS + j) * 2 + c, 1)].rearrange("b c h w -> h (b c) w")
                        chunk = (c * B + b) // CH
                        loaded = first_loaded[chunk] if isinstance(i, int) and i + j == 0 else x1_loaded[j]
                        sp.dma_start(x1[j][:, c, b:b + CH], src).then_inc(loaded, 16)

            def store_f(i, j, only=None):
                part = (j + 1) * UC if only is None else j * UC + (only + 1) * UC // 2
                sp.wait_ge(f_copied, i * BODY1 + part)
                for r in range(2):
                    for c in range(2) if only is None else (only,):
                        dst = f_dram[:, r, bass.ds((i * XS + j) * 2 + c, 1)].rearrange("g c y m -> y (g c) m")
                        src = f_sb[KH * r:KH * r + KH, j % 2, c].rearrange("p (g k) b -> p g (k b)", k=KG)
                        sp.dma_start(dst, src).then_inc(f_stored[j % 2], 16)

            def store_z(i):
                sp.wait_ge(z_copied, i + 1)
                dst = f64_dram[:, :, bass.ds(i * XS * 2, XS * 2), :].rearrange("r k c b -> (r k) c b")
                sp.dma_start(dst, zo_sb.rearrange("p (c b) -> p c b", b=B)).then_inc(z_stored, 16)

            def load_w(t_head, x0, slot):
                for r, w in enumerate((w_real, w_imag)):
                    src = w.rearrange("h i o x y -> h i o (x y)")[bass.ds(t_head, 1), :, :, bass.ds(x0 * KY, 2 * KY)]
                    sp.dma_start(w_sb[C * r:C * r + C, slot], src.rearrange("h i o m -> (h i) o m"))\
                        .then_inc(w_loaded[slot], 16)

            for j in range(XS):
                load_x1(0, j)
                if j == 1:
                    sp.dma_start(tab[:, :, :].rearrange("p t n -> p (t n)"), tables).then_inc(tab_loaded, 16)
            sp.wait_ge(bias_zeroed, 1)
            sp.dma_start(bias_col[0:CO], bias.rearrange("c a b -> c (a b)")).then_inc(bias_loaded, 16)
            with sp.Fori(0, ITER1 - 1) as i:
                for j in range(XS):
                    sp.wait_ge(t_done, (i * BODY1 + (j + 1) * UC) * 2)
                    load_x1(i + 1, j)
                    if j == XS - 1:
                        store_z(i)
                    store_f(i, j)
            def rows(t, i, j, lo, hi):
                return t[lo:hi, bass.ds(i * XS3 + j, 1)].rearrange("b c h w -> h (b c) w")

            def load_x3(i, j):
                for b in range(0, B, CH):
                    sp.dma_start(x3[:, j, b:b + CH], rows(x, i, j, b, b + CH)).then_inc(x3_loaded[j], 16)

            def load_planes(g, s):
                for r in range(2):
                    load_plane_rows(g, s, r, 0, C)
                    load_plane_nyquist(g, s, r)

            def load_plane_rows(g, s, r, lo, hi):
                dst = planes[C * (r ^ s) + lo:C * (r ^ s) + hi, 2 * s, 0:KH]
                src = f_dram[bass.ds(g, 1), r, lo:hi].rearrange("g c y m -> (g c) (y m)")
                sp.dma_start(dst.rearrange("p y k b -> p (y k b)"), src).then_inc(pl_loaded[s], 16)

            def load_plane_nyquist(g, s, r):
                src = f64_dram[r, bass.ds(g * KG, KG)].rearrange("k c b -> c k b")
                sp.dma_start(planes[C * (r ^ s):C * (r ^ s) + C, 2 * s, KH], src).then_inc(pl_loaded[s], 16)

            def store_g(i, m):
                sp.wait_ge(g_dve, (i * BODY2 + m + 1) * (GPQ // 2))
                sp.wait_ge(g_act, (i * BODY2 + m + 1) * (GPQ // 2))
                if isinstance(i, int) and i == 0 and m == 0:
                    sp.wait_ge(bias_added, 1)
                for k in range(2):
                    dst = g_dram[bass.ds((i * BODY2 + m) * 2 + k, 1)].rearrange("k r o m -> (k o) r m")
                    src = g_st[CO * k:CO * k + CO, m % 2].rearrange("p (r b) y -> p r (b y)", r=2)
                    sp.dma_start(dst, src).then_inc(g_stored[m % 2], 16)

            last = ITER1 - 1
            EARLY = C - 4
            store_f(last, 0)
            sp.wait_ge(t_done, (last * BODY1 + 2 * UC) * 2)
            store_f(last, 1)
            for a in range(2):
                sp.wait_ge(f_stored[a], 64 * ((XS // 2) * ITER1 - 1))
            for r in range(2):
                load_plane_rows(0, 0, r, 0, EARLY)
            sp.wait_ge(t_done, (last * BODY1 + 3 * UC) * 2)
            load_w(0, 0, 0)
            store_f(last, 2)
            for c in range(2):
                store_f(last, 3, c)
            store_z(last)
            for a in range(2):
                sp.wait_ge(f_stored[a], 64 * (XS // 2) * ITER1)
            sp.wait_ge(z_stored, 16 * ITER1)
            for r in range(2):
                load_plane_rows(0, 0, r, EARLY, C)
                load_plane_nyquist(0, 0, r)
            load_w(0, 2, 1)
            load_planes(1, 1)

            def mix_turn(i, m, head, x0, last):
                sp.wait_ge(mix_done, (i * BODY2 + m + 1) * GPQ)
                if not (last and m >= BODY2 - 2):
                    load_w(head, x0, m % 2)
                elif m == BODY2 - 2:
                    load_x3(0, 0)
                    load_x3(0, 1)
                if m % 2 and not last:
                    load_planes(i * 2 + 2 + m // 2, m // 2)
                store_g(i, m)

            def mix_body(i, head, half, last=False):
                for m in range(BODY2):
                    at = m + 2
                    if at < BODY2:
                        mix_turn(i, m, head, half * 2 * BODY2 + 2 * at, last)
                    elif half == 0:
                        mix_turn(i, m, head, 2 * BODY2 + 2 * (at - BODY2), last)
                    else:
                        mix_turn(i, m, head + 1, 2 * (at - BODY2), last)

            mix_body(0, 0, 0)
            mix_body(1, 0, 1)
            with sp.Fori(1, HEADS - 1) as hd:
                mix_body(hd * 2, hd, 0)
                mix_body(hd * 2 + 1, hd, 1)
            mix_body(ITER2 - 2, HEADS - 1, 0)
            mix_body(ITER2 - 1, HEADS - 1, 1, last=True)

            def load_g3(i, j):
                src = g_dram.rearrange("k r o m -> (k r) o m")[:, bass.ds(i * XS3 + j, 1)]
                sp.dma_start(g3[:, j].rearrange("p b y -> p (b y)"), src.rearrange("p o m -> p (o m)"))\
                    .then_inc(g3_loaded[j], 16)

            def store_out(i, j):
                sp.wait_ge(o_added, i * BODY3 + (j + 1) * UC3)
                sp.dma_start(rows(out, i, j, 0, B), x3[:, j]).then_inc(stored[j], 16)

            for s in range(2):
                sp.wait_ge(g_stored[s], 32 * (NQ // 2))
            for j in range(XS3):
                load_g3(0, j)
                if j % 2:
                    load_x3(0, 1 + (j + 1) // 2)

            with sp.Fori(0, ITER3 - 1) as i:
                for j in range(XS3):
                    sp.wait_ge(v_done, i * BODY3 + (j + 1) * UC3)
                    load_g3(i + 1, j)
                    store_out(i, j)
                    if j > 0:
                        sp.wait_ge(stored[j - 1], (i + 1) * 16)
                        load_x3(i + 1, j - 1)
                sp.wait_ge(stored[XS3 - 1], (i + 1) * 16)
                load_x3(i + 1, XS3 - 1)
            for j in range(XS3 - 1):
                store_out(ITER3 - 1, j)
            for n in range(UC3):
                sp.wait_ge(o_added, ITER3 * BODY3 - UC3 + n + 1)
                sp.dma_start(rows(out, ITER3 - 1, XS3 - 1, n * CH, n * CH + CH),
                             x3[:, XS3 - 1, n * CH:n * CH + CH]).then_inc(stored[XS3 - 1], 16)
            for j in range(XS3):
                sp.wait_ge(stored[j], 16 * (ITER3 if j < XS3 - 1 else ITER3 - 1 + UC3))

        STEPS = 18
        STEPS1 = 13

        @block.gpsimd
        def _(pool):
            NEG_MEAN, VAR, EPSILON, HALF, THREE_HALVES = range(5)
            for n, value in enumerate((-1.0 / (4 * P), 1.0 / (2 * H * W), EPS, -0.5, 1.5)):
                nc.gpsimd.memset(consts[:, n], value)
            nc.gpsimd.memset(seg_const[:, :, :, :], float(W // 2))
            nc.gpsimd.memset(fence[:, :], 0.0).then_inc(consts_ready, 1)
            pool.wait_ge(consts_ready, 1)

            def tt(o, a, b, op):
                return nc.gpsimd.tensor_tensor(o, a, b, op)

            def stepper(u, steps):
                def then(ins):
                    steps[0] += 1
                    ins.then_inc(pool_step, 1)
                    pool.wait_ge(pool_step, u * STEPS + steps[0])
                return then

            def carry_wait():
                tt(fence[:, 0:1], fence[:, 1:2], fence[:, 1:2], ALU.add)

            def statistics(i, j):
                s, u, steps = j % 2, i * XS + j, [0]
                then = stepper(u, steps)
                me_mo = st[:, s].rearrange("p c b (e v) -> p c b e v", e=2)[:, :, :, :, 1]
                m2 = st[:, s].rearrange("p c b (e v) -> p c b e v", e=2)[:, :, :, :, 2]
                pool.wait_ge(bn_done, u + 1)
                then(tt(msum2, me_mo[:, :, :, 0], me_mo[:, :, :, 1], ALU.add))
                then(tt(msum, msum2[:, 0], msum2[:, 1], ALU.add))
                carry_wait()
                then(nc.gpsimd.partition_all_reduce(sums, msum, P, bass.bass_isa.ReduceOp.add))
                then(tt(neg_mean, sums, consts[:, NEG_MEAN], ALU.mult))
                for e in range(2):
                    for c in range(2):
                        ins = tt(dev[:, c, :, e], me_mo[:, c, :, e], neg_mean, ALU.add)
                then(ins)
                then(tt(devsq, dev, dev, ALU.mult))
                then(tt(dev, devsq, seg_const, ALU.mult))
                then(tt(devsq, dev, m2, ALU.add))
                then(tt(qsum2, devsq[:, :, :, 0], devsq[:, :, :, 1], ALU.add))
                then(tt(qsum, qsum2[:, 0], qsum2[:, 1], ALU.add))
                carry_wait()
                then(nc.gpsimd.partition_all_reduce(sums, qsum, P, bass.bass_isa.ReduceOp.add))
                then(tt(var_n, sums, consts[:, VAR], ALU.mult))
                then(tt(var[:, s], var_n, consts[:, EPSILON], ALU.add))
                nc.gpsimd.tensor_tensor(fence[:, 0:1], fence[:, 1:2], fence[:, 1:2], ALU.add).then_inc(var_ready, 1)
                assert steps[0] == STEPS1, steps

            def scales(i, j, first=False):
                s, u, steps = j % 2, i * XS + j, [STEPS1]
                then = stepper(u, steps)
                me_mo = st[:, s].rearrange("p c b (e v) -> p c b e v", e=2)[:, :, :, :, 1]
                pool.wait_ge(rs0_ready, u + 1)
                then(tt(nt, rs0[:, s], rs0[:, s], ALU.mult))
                then(tt(nt2, nt, var[:, s], ALU.mult))
                then(tt(nt, nt2, consts[:, HALF], ALU.mult))
                then(tt(nt2, nt, consts[:, THREE_HALVES], ALU.add))
                wait(pool, norm_act, u - 1)
                then(tt(rstd[:, s], nt2, rs0[:, s], ALU.mult))
                tt(nbias[:, s], neg_mean, rstd[:, s], ALU.mult).then_inc(scale_ready, 1)
                pool.wait_ge(scale_ready, u + 1)
                tt(zdiff, me_mo[:, :, :, 0], me_mo[:, :, :, 1], ALU.subtract).then_inc(zdiff_ready, 1)
                for b in range(FIRST_D if first else NA, B):
                    v = x1[j][:, :, b]
                    ins = nc.gpsimd.tensor_scalar(v, v, rstd[:, s, b:b + 1], nbias[:, s, b:b + 1],
                                                  ALU.mult, ALU.add)
                ins.then_inc(norm_pool, 1)
                pool.wait_ge(zdiff_ready, u + 1)
                if j == 0:
                    wait(pool, z_done, i)
                for c in range(2):
                    ins = tt(z_sb[:, j, c], zdiff[:, c], rstd[:, s], ALU.mult)
                ins.then_inc(z_ready, 1)
                assert steps[0] == STEPS, steps

            def turn(i, j, first=False, last=False):
                scales(i, j, first)
                if not last:
                    statistics(*((i, j + 1) if j + 1 < XS else (i + 1, 0)))

            statistics(0, 0)
            for j in range(XS):
                turn(0, j, first=j == 0)
            with pool.Fori(1, ITER1 - 1) as i:
                for j in range(XS):
                    turn(i, j)
            for j in range(XS):
                turn(ITER1 - 1, j, last=j == XS - 1)

            pool.wait_ge(own_max_ready, 2)
            nc.gpsimd.partition_all_reduce(all_max, own_max, P, bass.bass_isa.ReduceOp.max).then_inc(all_max_ready, 1)

        @block.vector
        def _(dve):
            def after(i, j, n):
                return (i, j + n) if j + n < XS else (i + 1, j + n - XS)

            def stats(i, j, lo, hi, first=False):
                if lo == 0 and not first:
                    dve.wait_ge(x1_loaded[j], (i + (1 if j else 0)) * 16 * UC)
                    wait(dve, z_ready, i * XS + j - 1)
                for n in range(lo, hi):
                    if first and n % CH == 0:
                        dve.wait_ge(first_loaded[n // CH], 16)
                    ins = nc.vector.bn_stats(st[:, j % 2, n // B, n % B], x1[j][:, n // B, n % B])
                if hi == 2 * B:
                    ins.then_inc(bn_done, 1)

            def reciprocal(i, j):
                dve.wait_ge(sd_ready, i * XS + j + 1)
                nc.vector.reciprocal(rs0[:, j % 2], sd[:, j % 2]).then_inc(rs0_ready, 1)

            def low_part(i, hh):
                dve.wait_ge(t_high, i * BODY1 * 2 + hh + 1)
                b0 = hh % 2 * TH
                dst = t16[:, hh // 2 % TS, :, :, :, b0:b0 + TH].rearrange("p v r k b -> p v b r k")
                nc.vector.tensor_tensor(dst[:, 1], ps_t[hh % TS], dst[:, 0], ALU.subtract).then_inc(t_low, 1)

            def turn(i, j, left=XS):
                for n in range(UC):
                    for h in range(2):
                        low_part(i, (j * UC + n) * 2 + h)
                        if n == 0 and h == 0 and left > 1:
                            reciprocal(*after(i, j, 1))
                        at = n * CH + h * TH
                        if at < LEAD:
                            if left > 2:
                                lo = 2 * B - LEAD + at
                                stats(*after(i, j, 2), lo, lo + TH)
                        elif left > 3:
                            stats(*after(i, j, 3), at - LEAD, at - LEAD + TH)

            nc.vector.memset(bias_col, 0.0).then_inc(bias_zeroed, 1)
            stats(0, 0, 0, 2 * B, first=True)
            dve.wait_ge(tab_loaded, 16)
            for r, t in enumerate((dft_wr, dft_wi)):
                nc.vector.tensor_copy(dft_w16[:, r, 0], t).then_inc(split_ready, 1)
                dve.wait_ge(split_ready, 2 * r + 1)
                nc.vector.tensor_tensor(dft_w16[:, r, 1], t, dft_w16[:, r, 0], ALU.subtract).then_inc(split_ready, 1)
            nc.vector.tensor_copy(inv_w16[:, 0], inv_w).then_inc(split_ready, 1)
            dve.wait_ge(split_ready, 5)
            nc.vector.tensor_tensor(inv_w16[:, 1], inv_w, inv_w16[:, 0], ALU.subtract).then_inc(split_ready, 1)
            stats(0, 1, 0, 26)
            reciprocal(0, 0)
            stats(0, 1, 26, 40)
            dve.wait_ge(scale_ready, 1)
            for b in range(FIRST_A, FIRST_D):
                v = x1[0][:, :, b]
                ins = nc.vector.tensor_scalar(v, v, rstd[:, 0, b:b + 1], nbias[:, 0, b:b + 1], ALU.mult, ALU.add)
            ins.then_inc(norm_first, 1)
            stats(0, 1, 40, 2 * B)
            stats(0, 2, 0, 2 * B - LEAD)
            for j in range(XS):
                turn(0, j)
            with dve.Fori(1, ITER1 - 1) as i:
                for j in range(XS):
                    turn(i, j)
            for j in range(XS):
                turn(ITER1 - 1, j, left=XS - j)

            def build(i, m):
                s, k = m // 2, 2 * (m % 2)
                if m % 2 == 0:
                    dve.wait_ge(pl_loaded[s], (i + 1) * 64 + (0 if s else 32))
                wait(dve, mix_done, (i * BODY2 + m - 1) * GPQ)
                a = planes[0:C, 1, :, k:k + 2]
                b = planes[C:P, 2 * s, :, k:k + 2]
                ins = nc.vector.tensor_copy(a, b)
                if s == 0:
                    ins = nc.vector.tensor_scalar(b, b, -1.0, None, ALU.mult)
                ins.then_inc(pl_dve, 1)

            def weight_max(i, m, n):
                if n == 0:
                    dve.wait_ge(w_loaded[m % 2], i * 64 + (m // 2 + 1) * 32)
                if n == 0 and m == 0:
                    dve.wait_ge(w_run_ready, i + 1)
                piece = w_sb[:, m % 2, n * CO // WP:(n + 1) * CO // WP]
                at = m * WP + n
                nc.vector.tensor_reduce(w_max[:, at:at + 1], piece, mybir.AxisListType.XY, ALU.max,
                                        apply_absolute_value=True).then_inc(w_seen, 1)

            def keep_max(i):
                dve.wait_ge(w_seen, i * BODY2 * WP)
                dve.wait_ge(w_run_ready, i)
                nc.vector.tensor_tensor(w_run, w_run, w_max, ALU.max).then_inc(w_run_ready, 1)

            def copy_groups(i, m):
                wait(dve, g_stored[m % 2], i * 64 + (m // 2) * 32)
                for n in range(0, GPQ, 2):
                    k, y = n // (GPQ // 2), n % (GPQ // 2) * GK
                    dve.wait_ge(mix_done, (i * BODY2 + m) * GPQ + n + 1)
                    src = ps_g[(m * GPQ + n) % 4][C * k:C * k + C, 0:GK]
                    dst = g_st[C * k:C * k + C, m % 2, :, y:y + GK].rearrange("p n y -> p y n")
                    nc.vector.tensor_copy(dst, src).then_inc(g_dve, 1)
                    if n // 2 < WP:
                        weight_max(i, m, n // 2)

            def mix_turn(i, m, last=False):
                if not last:
                    build(*((i, m + 1) if m + 1 < BODY2 else (i + 1, 0)))
                copy_groups(i, m)

            nc.vector.memset(w_run, 0.0).then_inc(w_run_ready, 1)
            dve.wait_ge(bias_loaded, 16)
            nc.vector.tensor_scalar(bias_w, bias_col, float(W), None, ALU.mult).then_inc(bias_ready, 1)
            build(0, 0)
            for m in range(BODY2):
                mix_turn(0, m)
                if m == 0:
                    dve.wait_ge(g_dve, 1)
                    dve.wait_ge(bias_ready, 1)
                    dc = g_st[0:CO, 0, 0:B, 0]
                    nc.vector.tensor_scalar(dc, dc, bias_w[0:CO], None, ALU.add).then_inc(bias_added, 1)
            with dve.Fori(1, ITER2 - 1) as i:
                keep_max(i)
                for m in range(BODY2):
                    mix_turn(i, m)
            keep_max(ITER2 - 1)
            for m in range(BODY2):
                mix_turn(ITER2 - 1, m, m == BODY2 - 1)
            keep_max(ITER2)

            dve.wait_ge(w_run_ready, ITER2 + 1)
            nc.vector.tensor_reduce(own_max[:, 0:1], w_run, mybir.AxisListType.X, ALU.max).then_inc(own_max_ready, 1)
            nc.vector.tensor_reduce(own_max[:, 1:2], bias_col, mybir.AxisListType.X, ALU.max,
                                    apply_absolute_value=True).then_inc(own_max_ready, 1)
            dve.wait_ge(all_max_ready, 1)
            nc.vector.tensor_scalar(bound, all_max[:, 1:2], V_PER_BIAS, TINY, ALU.mult, ALU.add)\
                .then_inc(scale_step, 1)
            dve.wait_ge(scale_step, 1)
            nc.vector.scalar_tensor_tensor(out=bound_rec, in0=all_max[:, 0:1], scalar=V_PER_W, in1=bound,
                                           op0=ALU.mult, op1=ALU.add).then_inc(scale_step, 1)
            dve.wait_ge(scale_step, 2)
            nc.vector.tensor_scalar(v_unscale, bound_rec, 1.0 / (V_TOP * W_SCALE * W), None, ALU.mult)\
                .then_inc(scale_step, 1)
            nc.vector.reciprocal(bound, bound_rec).then_inc(scale_step, 1)
            dve.wait_ge(scale_step, 4)
            nc.vector.tensor_scalar(v_scale, bound, V_TOP, None, ALU.mult).then_inc(scale_step, 1)
            dve.wait_ge(scale_step, 5)

            def low_v(i, n):
                dve.wait_ge(v_high, i * BODY3 + n + 1)
                nc.vector.scalar_tensor_tensor(out=v16[:, n % 2, 1], in0=ps_v[n % 2], scalar=v_scale,
                                               in1=v16[:, n % 2, 0], op0=ALU.mult, op1=ALU.subtract)\
                    .then_inc(v_low, 1)

            def add_x(i, n):
                j, b0 = n // UC3, n % UC3 * CH
                if n % UC3 == 0:
                    dve.wait_ge(x3_loaded[j], (i + 1) * 16 * UC3)
                dve.wait_ge(o_done, i * BODY3 + n + 1)
                v = x3[:, j, b0:b0 + CH]
                nc.vector.scalar_tensor_tensor(out=v, in0=ps_o[n % 2], scalar=v_unscale, in1=v,
                                               op0=ALU.mult, op1=ALU.add).then_inc(o_added, 1)

            def out_body(i, first):
                for n in range(BODY3):
                    low_v(i, n)
                    if n:
                        add_x(i, n - 1)
                    elif not first:
                        add_x(i - 1, BODY3 - 1)

            out_body(0, True)
            with dve.Fori(1, ITER3) as i:
                out_body(i, False)
            add_x(ITER3 - 1, BODY3 - 1)

        @block.scalar
        def _(act):
            def root(i, j):
                act.wait_ge(var_ready, i * XS + j + 1)
                nc.scalar.activation(sd[:, j % 2], var[:, j % 2], ACT.Sqrt).then_inc(sd_ready, 1)

            def normalise(i, j, lo, hi):
                if lo == 0:
                    act.wait_ge(scale_ready, i * XS + j + 1)
                for b in range(lo, hi):
                    v = x1[j][:, :, b]
                    ins = nc.scalar.activation(v, v, ACT.Identity, bias=nbias[:, j % 2, b:b + 1],
                                               scale=rstd[:, j % 2, b:b + 1])
                if hi in (NA, FIRST_A):
                    ins.then_inc(norm_act, 1)

            def high_part(i, hh):
                act.wait_ge(t_done, i * BODY1 * 2 + hh + 1)
                m, h = hh // 2, hh % 2
                if h == 0:
                    wait(act, f_done, i * BODY1 + m + 1 - TS)
                dst = t16[:, m % TS, 0, :, :, h * TH:h * TH + TH].rearrange("p r k b -> p b r k")
                nc.scalar.activation(dst, ps_t[hh % TS], ACT.Copy).then_inc(t_high, 1)

            def copy_f(i, m):
                j, n = m // UC, m % UC
                if n == 0:
                    wait(act, f_stored[j % 2], (i * (XS // 2) + j // 2) * 64)
                act.wait_ge(f_done, i * BODY1 + m + 1)
                c, b0 = n // (UC // 2), n % (UC // 2) * CH
                src = ps_f[m % 2].rearrange("p (k b) -> p k b", b=CH)
                nc.scalar.activation(f_sb[:, j % 2, c, :, b0:b0 + CH], src, ACT.Copy,
                                     scale=1.0 / (T_SCALE * W_SCALE)).then_inc(f_copied, 1)

            def copy_z(i):
                act.wait_ge(z_done, i + 1)
                wait(act, z_stored, i * 16)
                nc.scalar.activation(zo_sb, ps_z, ACT.Copy).then_inc(z_copied, 1)

            NORM = [0, 0, 2, 4, 6, 8, 10, 12, NA]
            F_LAG = 3

            def turn(i, j, first=False, left=XS):
                nxt = (i, j + 1) if j + 1 < XS else (i + 1, 0)
                if left > 1:
                    root(*nxt)
                for n in range(UC):
                    m = j * UC + n
                    high_part(i, 2 * m)
                    high_part(i, 2 * m + 1)
                    if left > 1 and NORM[n + 1] > NORM[n]:
                        normalise(*nxt, NORM[n], NORM[n + 1])
                    if m >= F_LAG:
                        copy_f(i, m - F_LAG)
                    elif not first:
                        copy_f(i - 1, BODY1 + m - F_LAG)
                    if m == BODY1 - 1:
                        copy_z(i)

            root(0, 0)
            normalise(0, 0, 0, FIRST_A)
            for j in range(XS):
                turn(0, j, first=True)
            with act.Fori(1, ITER1 - 1) as i:
                for j in range(XS):
                    turn(i, j)
            for j in range(XS):
                turn(ITER1 - 1, j, left=XS - j)
            for m in range(BODY1 - F_LAG, BODY1):
                copy_f(ITER1 - 1, m)

            def build(i, m):
                s, k = m // 2, 2 * (m % 2)
                if m % 2 == 0:
                    act.wait_ge(pl_loaded[s], (i + 1) * 64 + (0 if s else 32))
                wait(act, mix_done, (i * BODY2 + m - 1) * GPQ)
                nc.scalar.activation(planes[C:P, 1, :, k:k + 2], planes[0:C, 2 * s, :, k:k + 2], ACT.Copy,
                                     scale=-1.0 if s else 1.0).then_inc(pl_act, 1)

            def copy_groups(i, m):
                wait(act, g_stored[m % 2], i * 64 + (m // 2) * 32)
                for n in range(1, GPQ, 2):
                    k, y = n // (GPQ // 2), n % (GPQ // 2) * GK
                    act.wait_ge(mix_done, (i * BODY2 + m) * GPQ + n + 1)
                    src = ps_g[(m * GPQ + n) % 4][C * k:C * k + C, 0:GK]
                    dst = g_st[C * k:C * k + C, m % 2, :, y:y + GK].rearrange("p n y -> p y n")
                    nc.scalar.activation(dst, src, ACT.Copy).then_inc(g_act, 1)

            def mix_turn(i, m, last=False):
                if not last:
                    build(*((i, m + 1) if m + 1 < BODY2 else (i + 1, 0)))
                copy_groups(i, m)

            build(0, 0)
            for m in range(BODY2):
                mix_turn(0, m)
            with act.Fori(1, ITER2 - 1) as i:
                for m in range(BODY2):
                    mix_turn(i, m)
            for m in range(BODY2):
                mix_turn(ITER2 - 1, m, m == BODY2 - 1)

            def high_v(i, n):
                act.wait_ge(v_done, i * BODY3 + n + 1)
                wait(act, o_done, i * BODY3 + n - 1)
                nc.scalar.activation(v16[:, n % 2, 0], ps_v[n % 2], ACT.Copy, scale=v_scale).then_inc(v_high, 1)

            act.wait_ge(scale_step, 5)
            for n in range(BODY3):
                high_v(0, n)
            with act.Fori(1, ITER3) as i:
                for n in range(BODY3):
                    high_v(i, n)

        @block.tensor
        def _(pe):
            def dft_rows(i, m):
                j, n = m // UC, m % UC
                if n == 0:
                    pe.wait_ge(norm_pool, i * XS + j + 1)
                    pe.wait_ge(norm_act, i * XS + j + 1)
                c, b0 = n // (UC // 2), n % (UC // 2) * CH
                for h in range(2):
                    wait(pe, t_low, (i * BODY1 + m) * 2 + h + 1 - TS)
                    for b in range(TH):
                        ins = nc.tensor.matmul(ps_t[(2 * m + h) % TS][:, b].rearrange("p r k -> p (r k)"),
                                               x1[j][:, c, b0 + h * TH + b], dft_h, start=True, stop=True)
                    ins.then_inc(t_done, 1)

            def dft_cols(i, m):
                pe.wait_ge(t_low, (i * BODY1 + m) * 2 + 2)
                wait(pe, f_copied, i * BODY1 + m - 1)
                terms = [(r, a, b) for r in range(2) for a, b in ((0, 0), (1, 0), (0, 1))]
                for n, (r, a, b) in enumerate(terms):
                    ins = nc.tensor.matmul(ps_f[m % 2], dft_w16[:, r, a],
                                           t16[:, m % TS, b, r].rearrange("p k b -> p (k b)"),
                                           start=(n == 0), stop=(n == len(terms) - 1))
                ins.then_inc(f_done, 1)

            def dft_nyquist(i):
                pe.wait_ge(z_ready, (i + 1) * XS)
                wait(pe, z_copied, i)
                nc.tensor.matmul(ps_z, dft_z, z_sb.rearrange("p a c b -> p (a c b)"),
                                 start=True, stop=True).then_inc(z_done, 1)

            LAG = 2

            def body(i, first):
                for m in range(BODY1):
                    if m == (XS - 1) * UC + 1:
                        dft_nyquist(i)
                    dft_rows(i, m)
                    if m >= LAG:
                        dft_cols(i, m - LAG)
                    elif not first:
                        dft_cols(i - 1, BODY1 + m - LAG)

            pe.wait_ge(tab_loaded, 16)
            pe.wait_ge(split_ready, 6)
            pe.wait_ge(norm_first, 1)
            body(0, True)
            with pe.Fori(1, ITER1) as i:
                body(i, False)
            for m in range(BODY1 - LAG, BODY1):
                dft_cols(ITER1 - 1, m)

            pe.wait_ge(f_copied, ITER1 * BODY1)
            pe.wait_ge(z_copied, ITER1)

            def mix_pair(i, m):
                s = m // 2
                pe.wait_ge(w_loaded[m % 2], i * 64 + (m // 2 + 1) * 32)
                pe.wait_ge(pl_dve, i * BODY2 + m + 1)
                pe.wait_ge(pl_act, i * BODY2 + m + 1)
                for n in range(GPQ):
                    seen = (m * GPQ + n) // 2 - 1
                    wait(pe, g_dve if n % 2 == 0 else g_act, i * (BODY2 * GPQ // 2) + seen)
                    k, y0 = n // (GPQ // 2), n % (GPQ // 2) * GK
                    if n == GPQ - 1:
                        pe.wait_ge(w_seen, (i * BODY2 + m + 1) * WP)
                    for y in range(GK):
                        ins = nc.tensor.matmul(ps_g[(m * GPQ + n) % 4][C * k:C * k + C, y],
                                               w_sb[:, m % 2, :, k * KY + y0 + y],
                                               planes[:, s:s + 2, y0 + y, 2 * (m % 2) + k, :],
                                               start=True, stop=True)
                    ins.then_inc(mix_done, 1)

            for m in range(BODY2):
                mix_pair(0, m)
            with pe.Fori(1, ITER2) as i:
                for m in range(BODY2):
                    mix_pair(i, m)

            pe.wait_ge(g_dve, NQ * GPQ // 2)
            pe.wait_ge(g_act, NQ * GPQ // 2)

            def inverse_rows(i, n):
                j, b0 = n // UC3, n % UC3 * CH
                if n % UC3 == 0:
                    pe.wait_ge(g3_loaded[j], i * 16 + 16)
                wait(pe, v_low, i * BODY3 + n - 1)
                for c in range(CH):
                    for r, t in enumerate((inv_r, inv_i)):
                        ins = nc.tensor.matmul(ps_v[n % 2][KH * r:KH * r + KH, c], g3[:, j, b0 + c, r:r + KH], t,
                                               start=True, stop=True)
                ins.then_inc(v_done, 1)

            def inverse_cols(i, n):
                pe.wait_ge(v_low, i * BODY3 + n + 1)
                wait(pe, o_added, i * BODY3 + n - 1)
                for c in range(CH):
                    for t, (a, b) in enumerate(((0, 0), (0, 1), (1, 0))):
                        ins = nc.tensor.matmul(ps_o[n % 2][:, c], v16[:, n % 2, a, c], inv_w16[:, b],
                                               start=(t == 0), stop=(t == 2))
                ins.then_inc(o_done, 1)

            def inverse_body(i, first):
                for n in range(BODY3):
                    inverse_rows(i, n)
                    if n:
                        inverse_cols(i, n - 1)
                    elif not first:
                        inverse_cols(i - 1, BODY3 - 1)

            inverse_body(0, True)
            with pe.Fori(1, ITER3) as i:
                inverse_body(i, False)
            inverse_cols(ITER3 - 1, BODY3 - 1)


def dft_tables(n, kx, ky):
    import numpy as np

    a = 2 * np.pi / n
    p = np.arange(n)[:, None]
    k = np.arange(kx)[None, :]
    c, s = np.cos(a * p * k), np.sin(a * p * k)
    dft_h = np.concatenate([c, -s], 1) / n * 2048
    dft_wr = np.concatenate([c, -s], 1) * 256
    dft_wi = np.concatenate([s, c], 1) * 256
    dft_z = np.concatenate([s, c], 1) / n * (n // 2)
    h = np.arange(n)[None, :]
    kk = np.arange(kx)[:, None]
    c, s = np.cos(a * kk * h), np.sin(a * kk * h)
    inv_r = np.stack([c, -s], 1).reshape(2 * kx, n)
    inv_i = np.stack([s, c], 1).reshape(2 * kx, n)
    y = np.arange(ky)[:, None]
    cy, sy = np.cos(a * y * h), np.sin(a * y * h)
    weight = np.where((y == 0) | (y == ky - 1), 1.0, 2.0) * 256
    inv_w = np.concatenate([(weight * cy)[:ky - 1], (-weight * sy)[1:ky - 1], (weight * cy)[ky - 1:]], 0)
    return np.ascontiguousarray(np.concatenate([dft_h, dft_wr, dft_wi, dft_z, inv_r, inv_i, inv_w], 1), np.float32)


_INS = ["x", "L0_conv_weights_real", "L0_conv_weights_imag", "L0_conv_bias"]


def kernel(**inputs):
    import numpy as _np
    import concourse.bacc as _bacc
    from concourse import mybir as _mybir
    from concourse.bass_utils import run_bass_kernel_spmd as _run

    nc = _bacc.Bacc("TRN2", target_bir_lowering=False, num_devices=1)
    arrays, args = {}, []
    for name in _INS:
        arrays[f"in_{name}_dram"] = _np.ascontiguousarray(inputs[name])
    n = inputs["x"].shape[-1]
    arrays["in_tables_dram"] = dft_tables(n, n // 2, n // 2 + 1)
    for name, a in arrays.items():
        args.append(nc.dram_tensor(name, a.shape, _mybir.dt.from_np(a.dtype), kind="ExternalInput").ap())
    shape = tuple(inputs["x"].shape)
    args.append(nc.dram_tensor("out_0_dram", shape, _mybir.dt.float32, kind="ExternalOutput").ap())
    spectral_conv_kernel(nc, *args)
    r = _run(nc, [arrays], core_ids=[0])
    return r.results[0]["out_0_dram"]
```

```python
import concourse.bass as bass
from concourse import mybir
from contextlib import ExitStack


def spectral_conv_kernel(nc, x, w_real, w_imag, bias, tables, out):
    fp32 = mybir.dt.float32
    fp16 = mybir.dt.float16
    ALU = mybir.AluOpType
    ACT = mybir.ActivationFunctionType

    B, C, H, W = x.shape
    HEADS, _, CO, MX, KY = w_real.shape
    KX = HEADS * MX
    KH = KY - 1
    P = 128
    EPS = 1e-5

    XS = 4
    CH = 8
    TH = CH // 2
    UC = 2 * B // CH
    BODY1 = XS * UC
    ITER1 = C // 2 // XS
    TS = 4
    NA = 12
    FIRST_A, FIRST_D = 9, 24
    EARLY_ROOTS = [3, 3, 2, 1]
    LEAD = 5 * CH
    T_SCALE = 2048.0
    W_SCALE = 256.0
    KG = 4
    NG = KX // KG
    NQ = KX // 2
    BODY2 = 4
    ITER2 = NQ // BODY2
    GK = 13
    GPQ = 2 * KY // GK
    FIRST_PARTS = 4 * 16
    WP = 4
    XS3 = 4
    UC3 = B // CH
    BODY3 = XS3 * UC3
    ITER3 = CO // XS3
    V_TOP = 32768.0
    V_PER_W = float(C * H * W) ** 0.5 * float(2 * C * KX) ** 0.5
    V_PER_BIAS = float(W)
    TINY = 1e-30

    ctx = ExitStack()
    with ctx:
        def sem(name):
            return ctx.enter_context(nc.semaphore(name))

        f_dram = nc.dram_tensor("f_spectrum", (NG, 2, C, KH, KG * B), fp32, kind="Internal").ap()
        f64_dram = nc.dram_tensor("f_nyquist", (2, KX, C, B), fp32, kind="Internal").ap()
        g_dram = nc.dram_tensor("g_spectrum", (KX, 2, CO, B * KY), fp32, kind="Internal").ap()

        NT = tables.shape[1] // P
        tab = ctx.enter_context(nc.sbuf_tensor("tab", [P, NT, P], fp32))
        dft_h, dft_wr, dft_wi, dft_z, inv_r, inv_i, inv_w = (tab[:, n, :] for n in range(NT))
        dft_w16 = ctx.enter_context(nc.sbuf_tensor("dft_w16", [P, 2, 2, P], fp16))
        wring = ctx.enter_context(nc.sbuf_tensor("wring", [P, 2 * CO * 2 * KY], fp32))
        arena = ctx.enter_context(nc.sbuf_tensor("arena", [P, 3 * KY * KG * B + 2 * 2 * B * KY], fp32))
        inv_w16 = ctx.enter_context(nc.sbuf_tensor("inv_w16", [P, 2, P], fp16))
        small = ctx.enter_context(nc.sbuf_tensor("small", [P, 2 * BODY2 * WP + 10], fp32))
        w_max, w_run = small[:, 0:BODY2 * WP], small[:, BODY2 * WP:2 * BODY2 * WP]
        own_max, all_max, bias_col, bias_w, bound, bound_rec, v_scale, v_unscale = (
            small[:, 2 * BODY2 * WP + a:2 * BODY2 * WP + b]
            for a, b in ((0, 2), (2, 4), (4, 5), (5, 6), (6, 7), (7, 8), (8, 9), (9, 10)))

        w_sb = wring[:, :].rearrange("p (s o m) -> p s o m", s=2, o=CO)
        used = 0

        def carve(n):
            nonlocal used
            used += n
            return arena[:, used - n:used]

        def pairs(t):
            return t.rearrange("p (c b) -> p c b", c=2)

        half = 2 * B * W
        PLANE = KY * KG * B
        x1 = [t.rearrange("p (c b w) -> p c b w", c=2, b=B)
              for t in (wring[:, 0:half], wring[:, wring.shape[1] - half:], carve(PLANE)[:, 0:half],
                        carve(PLANE)[:, PLANE - half:])]
        t16 = carve(TS * CH * P).bitcast(fp16).rearrange("p (s v r k b) -> p s v r k b", s=TS, v=2, r=2, k=KX)
        f_sb = carve(2 * 2 * KX * B).rearrange("p (s c k b) -> p s c k b", s=2, c=2, k=KX)
        st = carve(2 * 2 * B * 6).rearrange("p (s c b v) -> p s c b v", s=2, c=2, b=B)
        z_sb = carve(XS * 2 * B).rearrange("p (a c b) -> p a c b", a=XS, c=2)
        zo_sb = carve(XS * 2 * B)
        msum2, qsum2, zdiff = pairs(carve(2 * B)), pairs(carve(2 * B)), pairs(carve(2 * B))
        dev = carve(4 * B).rearrange("p (c b v) -> p c b v", c=2, v=2)
        devsq = carve(4 * B).rearrange("p (c b v) -> p c b v", c=2, v=2)
        msum, qsum, sums, neg_mean, var_n, nt, nt2 = (carve(B) for _ in range(7))
        var, sd, rs0, rstd, nbias = (pairs(carve(2 * B)) for _ in range(5))
        seg_const = carve(4 * B).rearrange("p (c b v) -> p c b v", c=2, v=2)
        consts = carve(5 * B).rearrange("p (n m) -> p n m", n=5)
        fence = carve(2)
        assert used <= arena.shape[1]
        used = 0
        planes = carve(3 * PLANE).rearrange("p (s y k b) -> p s y k b", s=3, y=KY, k=KG)
        g_st = carve(2 * 2 * B * KY).rearrange("p (s n y) -> p s n y", s=2, n=2 * B)
        used = 0
        g3 = carve(XS3 * B * KY).rearrange("p (s b y) -> p s b y", s=XS3, b=B)
        v16 = carve(2 * CH * H).bitcast(fp16).rearrange("p (s v b h) -> p s v b h", s=2, v=2, b=CH)
        x3 = wring[:, 0:XS3 * B * W].rearrange("p (s b w) -> p s b w", s=XS3, b=B)

        ps = ctx.enter_context(nc.psum_tensor("ps", [P, 8, 512], fp32))
        ps_t = [ps[:, s, :].rearrange("p (i r k) -> p i r k", r=2, k=KX) for s in range(TS)]
        ps_f = [ps[:, TS + s, :] for s in range(2)]
        ps_z = ps[:, TS + 2, 0:XS * 2 * B]
        ps_g = [ps[:, 2 * s:2 * s + 2, :].rearrange("p a (y n) -> p (a y) n", n=2 * B) for s in range(4)]
        ps_v = [ps[:, 2 * s:2 * s + 2, :].rearrange("p a (i h) -> p (a i) h", h=H) for s in range(2)]
        ps_o = [ps[:, 4 + 2 * s:6 + 2 * s, :].rearrange("p a (i h) -> p (a i) h", h=H) for s in range(2)]

        tab_loaded = sem("tab_loaded")
        bias_zeroed = sem("bias_zeroed")
        bias_loaded = sem("bias_loaded")
        bias_ready = sem("bias_ready")
        early_loaded = [[sem(f"early_loaded{j}_{n}") for n in range(UC)] for j in range(2)]
        x1_loaded = [sem(f"x1_loaded{s}") for s in range(XS)]
        consts_ready = sem("consts_ready")
        bn_done = sem("bn_done")
        pool_step = sem("pool_step")
        var_ready = sem("var_ready")
        sd_ready = sem("sd_ready")
        rs0_ready = sem("rs0_ready")
        scale_ready = sem("scale_ready")
        zdiff_ready = sem("zdiff_ready")
        z_ready = sem("z_ready")
        split_ready = sem("split_ready")
        norm_first = sem("norm_first")
        norm_pool = sem("norm_pool")
        norm_act = sem("norm_act")
        t_done = sem("t_done")
        t_high = sem("t_high")
        t_low = sem("t_low")
        f_done = sem("f_done")
        f_copied = sem("f_copied")
        z_done = sem("z_done")
        z_copied = sem("z_copied")
        f_stored = [sem(f"f_stored{s}") for s in range(2)]
        z_stored = sem("z_stored")
        w_loaded = [sem(f"w_loaded{s}") for s in range(2)]
        pl_loaded = [sem(f"pl_loaded{s}") for s in range(2)]
        pl_dve = sem("pl_dve")
        pl_act = sem("pl_act")
        first_kx = sem("first_kx")
        mix_done = sem("mix_done")
        w_seen = sem("w_seen")
        w_run_ready = sem("w_run_ready")
        own_max_ready = sem("own_max_ready")
        all_max_ready = sem("all_max_ready")
        scale_step = sem("scale_step")
        bias_added = sem("bias_added")
        g_dve = sem("g_dve")
        g_act = sem("g_act")
        g_stored = [sem(f"g_stored{s}") for s in range(2)]
        x3_loaded = [sem(f"x3_loaded{s}") for s in range(XS3)]
        g3_loaded = [sem(f"g3_loaded{s}") for s in range(XS3)]
        v_done = sem("v_done")
        v_high = sem("v_high")
        v_low = sem("v_low")
        o_done = sem("o_done")
        o_added = sem("o_added")
        stored = [sem(f"stored{s}") for s in range(XS3)]

        block = ctx.enter_context(nc.Block())

        def wait(e, s, value):
            if not isinstance(value, int) or value > 0:
                e.wait_ge(s, value)

        @block.sync
        def _(sp):
            def load_x1(i, j):
                for c in range(2):
                    for b in range(0, B, CH):
                        src = x[b:b + CH, bass.ds((i * XS + j) * 2 + c, 1)].rearrange("b c h w -> h (b c) w")
                        chunk = (c * B + b) // CH
                        loaded = early_loaded[j][chunk] if isinstance(i, int) and j < 2 else x1_loaded[j]
                        sp.dma_start(x1[j][:, c, b:b + CH], src).then_inc(loaded, 16)

            def store_f(i, j, only=None):
                part = (j + 1) * UC if only is None else j * UC + (only + 1) * UC // 2
                sp.wait_ge(f_copied, i * BODY1 + part)
                for r in range(2):
                    for c in range(2) if only is None else (only,):
                        dst = f_dram[:, r, bass.ds((i * XS + j) * 2 + c, 1)].rearrange("g c y m -> y (g c) m")
                        src = f_sb[KH * r:KH * r + KH, j % 2, c].rearrange("p (g k) b -> p g (k b)", k=KG)
                        sp.dma_start(dst, src).then_inc(f_stored[j % 2], 16)

            def store_z(i):
                sp.wait_ge(z_copied, i + 1)
                dst = f64_dram[:, :, bass.ds(i * XS * 2, XS * 2), :].rearrange("r k c b -> (r k) c b")
                sp.dma_start(dst, zo_sb.rearrange("p (c b) -> p c b", b=B)).then_inc(z_stored, 16)

            def load_w(t_head, x0, slot):
                for r, w in enumerate((w_real, w_imag)):
                    src = w.rearrange("h i o x y -> h i o (x y)")[bass.ds(t_head, 1), :, :, bass.ds(x0 * KY, 2 * KY)]
                    sp.dma_start(w_sb[C * r:C * r + C, slot], src.rearrange("h i o m -> (h i) o m"))\
                        .then_inc(w_loaded[slot], 16)

            for j in range(XS):
                load_x1(0, j)
                if j == 0:
                    sp.dma_start(tab[:, :, :].rearrange("p t n -> p (t n)"), tables).then_inc(tab_loaded, 16)
            sp.wait_ge(bias_zeroed, 1)
            sp.dma_start(bias_col[0:CO], bias.rearrange("c a b -> c (a b)")).then_inc(bias_loaded, 16)
            with sp.Fori(0, ITER1 - 1) as i:
                for j in range(XS):
                    sp.wait_ge(t_done, (i * BODY1 + (j + 1) * UC) * 2)
                    load_x1(i + 1, j)
                    if j == XS - 1:
                        store_z(i)
                    store_f(i, j)
            def rows(t, i, j, lo, hi):
                return t[lo:hi, bass.ds(i * XS3 + j, 1)].rearrange("b c h w -> h (b c) w")

            def load_x3(i, j, lo=0, hi=B):
                for b in range(lo, hi, CH):
                    sp.dma_start(x3[:, j, b:b + CH], rows(x, i, j, b, b + CH)).then_inc(x3_loaded[j], 16)

            def load_planes(g, s):
                for r in range(2):
                    load_plane_rows(g, s, r, 0, C)
                    load_plane_nyquist(g, s, r)

            def load_plane_rows(g, s, r, lo, hi):
                dst = planes[C * (r ^ s) + lo:C * (r ^ s) + hi, s, 0:KH]
                src = f_dram[bass.ds(g, 1), r, lo:hi].rearrange("g c y m -> (g c) (y m)")
                sp.dma_start(dst.rearrange("p y k b -> p (y k b)"), src).then_inc(pl_loaded[s], 16)

            def load_plane_nyquist(g, s, r):
                src = f64_dram[r, bass.ds(g * KG, KG)].rearrange("k c b -> c k b")
                sp.dma_start(planes[C * (r ^ s):C * (r ^ s) + C, s, KH], src).then_inc(pl_loaded[s], 16)

            def g_copied(i, m, kxs):
                groups = kxs * (GPQ // 2)
                sp.wait_ge(g_dve, (i * BODY2 + m) * (GPQ // 2) + (groups + 1) // 2)
                sp.wait_ge(g_act, (i * BODY2 + m) * (GPQ // 2) + groups // 2)

            def store_g(i, m, final=False):
                if not final:
                    g_copied(i, m, 2)
                if isinstance(i, int) and i == 0 and m == 0:
                    sp.wait_ge(bias_added, 1)
                for k in range(2):
                    if final:
                        g_copied(i, m, k + 1)
                    dst = g_dram[bass.ds((i * BODY2 + m) * 2 + k, 1)].rearrange("k r o m -> (k o) r m")
                    src = g_st[CO * k:CO * k + CO, m % 2].rearrange("p (r b) y -> p r (b y)", r=2)
                    sp.dma_start(dst, src).then_inc(g_stored[m % 2], 16)

            last = ITER1 - 1
            sp.wait_ge(t_done, (last * BODY1 + UC) * 2)
            load_w(0, 0, 0)
            store_f(last, 0)
            sp.wait_ge(t_done, (last * BODY1 + 2 * UC) * 2)
            load_w(0, 2, 1)
            store_f(last, 1)
            sp.wait_ge(t_done, (last * BODY1 + 3 * UC) * 2)
            for a in range(2):
                sp.wait_ge(f_stored[a], 64 * ((XS // 2) * ITER1 - 1))
            for r in range(2):
                load_plane_rows(0, 0, r, 0, C - 4)
            store_f(last, 2)
            store_f(last, 3, 0)
            sp.wait_ge(f_stored[0], 64 * (XS // 2) * ITER1)
            for r in range(2):
                load_plane_rows(0, 0, r, C - 4, C - 2)
            store_f(last, 3, 1)
            store_z(last)
            sp.wait_ge(f_stored[1], 64 * (XS // 2) * ITER1)
            sp.wait_ge(z_stored, 16 * ITER1)
            for r in range(2):
                load_plane_rows(0, 0, r, C - 2, C)
                load_plane_nyquist(0, 0, r)
            load_planes(1, 1)

            def mix_turn(i, m, head, x0, last):
                if not (last and m == BODY2 - 1):
                    sp.wait_ge(mix_done, (i * BODY2 + m + 1) * GPQ)
                if not (last and m >= BODY2 - 2):
                    load_w(head, x0, m % 2)
                elif m == BODY2 - 2:
                    load_x3(0, 0)
                    load_x3(0, 1, 0, B // 2)
                if m % 2 and not last:
                    load_planes(i * 2 + 2 + m // 2, m // 2)
                store_g(i, m, last and m == BODY2 - 1)

            def mix_body(i, head, half, last=False):
                for m in range(BODY2):
                    at = m + 2
                    if at < BODY2:
                        mix_turn(i, m, head, half * 2 * BODY2 + 2 * at, last)
                    elif half == 0:
                        mix_turn(i, m, head, 2 * BODY2 + 2 * (at - BODY2), last)
                    else:
                        mix_turn(i, m, head + 1, 2 * (at - BODY2), last)

            mix_body(0, 0, 0)
            mix_body(1, 0, 1)
            with sp.Fori(1, HEADS - 1) as hd:
                mix_body(hd * 2, hd, 0)
                mix_body(hd * 2 + 1, hd, 1)
            mix_body(ITER2 - 2, HEADS - 1, 0)
            mix_body(ITER2 - 1, HEADS - 1, 1, last=True)

            def load_g3(i, j):
                src = g_dram.rearrange("k r o m -> (k r) o m")[:, bass.ds(i * XS3 + j, 1)]
                sp.dma_start(g3[:, j].rearrange("p b y -> p (b y)"), src.rearrange("p o m -> p (o m)"))\
                    .then_inc(g3_loaded[j], 16)

            def store_out(i, j):
                sp.wait_ge(o_added, i * BODY3 + (j + 1) * UC3)
                sp.dma_start(rows(out, i, j, 0, B), x3[:, j]).then_inc(stored[j], 16)

            load_x3(0, 1, B // 2, B)
            for s in range(2):
                sp.wait_ge(g_stored[s], 32 * (NQ // 2))
            for j in range(XS3):
                load_g3(0, j)
                if j % 2:
                    load_x3(0, 1 + (j + 1) // 2)

            with sp.Fori(0, ITER3 - 1) as i:
                for j in range(XS3):
                    sp.wait_ge(v_done, i * BODY3 + (j + 1) * UC3)
                    load_g3(i + 1, j)
                    store_out(i, j)
                    if j > 0:
                        sp.wait_ge(stored[j - 1], (i + 1) * 16)
                        load_x3(i + 1, j - 1)
                sp.wait_ge(stored[XS3 - 1], (i + 1) * 16)
                load_x3(i + 1, XS3 - 1)
            for j in range(XS3 - 1):
                store_out(ITER3 - 1, j)
            for n in range(UC3):
                sp.wait_ge(o_added, ITER3 * BODY3 - UC3 + n + 1)
                sp.dma_start(rows(out, ITER3 - 1, XS3 - 1, n * CH, n * CH + CH),
                             x3[:, XS3 - 1, n * CH:n * CH + CH]).then_inc(stored[XS3 - 1], 16)
            for j in range(XS3):
                sp.wait_ge(stored[j], 16 * (ITER3 if j < XS3 - 1 else ITER3 - 1 + UC3))

        STEPS = 18
        STEPS1 = 13

        @block.gpsimd
        def _(pool):
            NEG_MEAN, VAR, EPSILON, HALF, THREE_HALVES = range(5)
            for n, value in enumerate((-1.0 / (4 * P), 1.0 / (2 * H * W), EPS, -0.5, 1.5)):
                nc.gpsimd.memset(consts[:, n], value)
            nc.gpsimd.memset(seg_const[:, :, :, :], float(W // 2))
            nc.gpsimd.memset(fence[:, :], 0.0).then_inc(consts_ready, 1)
            pool.wait_ge(consts_ready, 1)

            def tt(o, a, b, op):
                return nc.gpsimd.tensor_tensor(o, a, b, op)

            def stepper(u, steps):
                def then(ins):
                    steps[0] += 1
                    ins.then_inc(pool_step, 1)
                    pool.wait_ge(pool_step, u * STEPS + steps[0])
                return then

            def carry_wait():
                tt(fence[:, 0:1], fence[:, 1:2], fence[:, 1:2], ALU.add)

            def statistics(i, j):
                s, u, steps = j % 2, i * XS + j, [0]
                then = stepper(u, steps)
                me_mo = st[:, s].rearrange("p c b (e v) -> p c b e v", e=2)[:, :, :, :, 1]
                m2 = st[:, s].rearrange("p c b (e v) -> p c b e v", e=2)[:, :, :, :, 2]
                pool.wait_ge(bn_done, u + 1)
                then(tt(msum2, me_mo[:, :, :, 0], me_mo[:, :, :, 1], ALU.add))
                then(tt(msum, msum2[:, 0], msum2[:, 1], ALU.add))
                carry_wait()
                then(nc.gpsimd.partition_all_reduce(sums, msum, P, bass.bass_isa.ReduceOp.add))
                then(tt(neg_mean, sums, consts[:, NEG_MEAN], ALU.mult))
                for e in range(2):
                    for c in range(2):
                        ins = tt(dev[:, c, :, e], me_mo[:, c, :, e], neg_mean, ALU.add)
                then(ins)
                then(tt(devsq, dev, dev, ALU.mult))
                then(tt(dev, devsq, seg_const, ALU.mult))
                then(tt(devsq, dev, m2, ALU.add))
                then(tt(qsum2, devsq[:, :, :, 0], devsq[:, :, :, 1], ALU.add))
                then(tt(qsum, qsum2[:, 0], qsum2[:, 1], ALU.add))
                carry_wait()
                then(nc.gpsimd.partition_all_reduce(sums, qsum, P, bass.bass_isa.ReduceOp.add))
                then(tt(var_n, sums, consts[:, VAR], ALU.mult))
                then(tt(var[:, s], var_n, consts[:, EPSILON], ALU.add))
                nc.gpsimd.tensor_tensor(fence[:, 0:1], fence[:, 1:2], fence[:, 1:2], ALU.add).then_inc(var_ready, 1)
                assert steps[0] == STEPS1, steps

            def scales(i, j, first=False):
                s, u, steps = j % 2, i * XS + j, [STEPS1]
                then = stepper(u, steps)
                me_mo = st[:, s].rearrange("p c b (e v) -> p c b e v", e=2)[:, :, :, :, 1]
                pool.wait_ge(rs0_ready, u + 1)
                then(tt(nt, rs0[:, s], rs0[:, s], ALU.mult))
                then(tt(nt2, nt, var[:, s], ALU.mult))
                then(tt(nt, nt2, consts[:, HALF], ALU.mult))
                then(tt(nt2, nt, consts[:, THREE_HALVES], ALU.add))
                wait(pool, norm_act, u - 1)
                then(tt(rstd[:, s], nt2, rs0[:, s], ALU.mult))
                tt(nbias[:, s], neg_mean, rstd[:, s], ALU.mult).then_inc(scale_ready, 1)
                pool.wait_ge(scale_ready, u + 1)
                tt(zdiff, me_mo[:, :, :, 0], me_mo[:, :, :, 1], ALU.subtract).then_inc(zdiff_ready, 1)
                for b in range(FIRST_D if first else NA, B):
                    v = x1[j][:, :, b]
                    ins = nc.gpsimd.tensor_scalar(v, v, rstd[:, s, b:b + 1], nbias[:, s, b:b + 1],
                                                  ALU.mult, ALU.add)
                ins.then_inc(norm_pool, 1)
                pool.wait_ge(zdiff_ready, u + 1)
                if j == 0:
                    wait(pool, z_done, i)
                for c in range(2):
                    ins = tt(z_sb[:, j, c], zdiff[:, c], rstd[:, s], ALU.mult)
                ins.then_inc(z_ready, 1)
                assert steps[0] == STEPS, steps

            def turn(i, j, first=False, last=False):
                scales(i, j, first)
                if not last:
                    statistics(*((i, j + 1) if j + 1 < XS else (i + 1, 0)))

            statistics(0, 0)
            for j in range(XS):
                turn(0, j, first=j == 0)
            with pool.Fori(1, ITER1 - 1) as i:
                for j in range(XS):
                    turn(i, j)
            for j in range(XS):
                turn(ITER1 - 1, j, last=j == XS - 1)

            pool.wait_ge(own_max_ready, 2)
            nc.gpsimd.partition_all_reduce(all_max, own_max, P, bass.bass_isa.ReduceOp.max).then_inc(all_max_ready, 1)

        @block.vector
        def _(dve):
            def after(i, j, n):
                return (i, j + n) if j + n < XS else (i + 1, j + n - XS)

            def stats(i, j, lo, hi, early=False):
                if lo == 0 and not early:
                    dve.wait_ge(x1_loaded[j], (i + (0 if j < 2 else 1)) * 16 * UC)
                    wait(dve, z_ready, i * XS + j - 1)
                for n in range(lo, hi):
                    if early and (n % CH == 0 or n == lo):
                        dve.wait_ge(early_loaded[j][n // CH], 16)
                    ins = nc.vector.bn_stats(st[:, j % 2, n // B, n % B], x1[j][:, n // B, n % B])
                if hi == 2 * B:
                    ins.then_inc(bn_done, 1)

            def reciprocal(i, j):
                dve.wait_ge(sd_ready, i * XS + j + 1)
                nc.vector.reciprocal(rs0[:, j % 2], sd[:, j % 2]).then_inc(rs0_ready, 1)

            def low_part(i, hh):
                dve.wait_ge(t_high, i * BODY1 * 2 + hh + 1)
                b0 = hh % 2 * TH
                dst = t16[:, hh // 2 % TS, :, :, :, b0:b0 + TH].rearrange("p v r k b -> p v b r k")
                nc.vector.tensor_tensor(dst[:, 1], ps_t[hh % TS], dst[:, 0], ALU.subtract).then_inc(t_low, 1)

            AHEAD = 2 * B - LEAD

            def turn(i, j, root_at=0, begin=AHEAD, end=AHEAD, left=XS):
                halves = 2 * UC
                count = 2 * B - begin + end
                for hh in range(halves):
                    if hh == 2 * root_at and left > 1:
                        reciprocal(*after(i, j, 1))
                    low_part(i, j * halves + hh)
                    lo, hi = (begin + count * (hh + k) // halves for k in range(2))
                    if lo < 2 * B and left > 2:
                        stats(*after(i, j, 2), lo, min(hi, 2 * B))
                    if hi > 2 * B and left > 3:
                        stats(*after(i, j, 3), max(lo - 2 * B, 0), hi - 2 * B)
                    if left <= 2 and hh % 4 == 3:
                        weight_max(0, 2 - left, hh // 4)

            def weight_max(i, m, n):
                if n == 0:
                    dve.wait_ge(w_loaded[m % 2], i * 64 + (m // 2 + 1) * 32)
                if n == 0 and m == 0:
                    dve.wait_ge(w_run_ready, i + 1)
                piece = w_sb[:, m % 2, n * CO // WP:(n + 1) * CO // WP]
                at = m * WP + n
                nc.vector.tensor_reduce(w_max[:, at:at + 1], piece, mybir.AxisListType.XY, ALU.max,
                                        apply_absolute_value=True).then_inc(w_seen, 1)

            nc.vector.memset(bias_col, 0.0).then_inc(bias_zeroed, 1)
            nc.vector.memset(w_run, 0.0).then_inc(w_run_ready, 1)
            stats(0, 0, 0, 2 * B, early=True)
            dve.wait_ge(tab_loaded, 16)
            for r, t in enumerate((dft_wr, dft_wi)):
                nc.vector.tensor_copy(dft_w16[:, r, 0], t).then_inc(split_ready, 1)
                dve.wait_ge(split_ready, 2 * r + 1)
                nc.vector.tensor_tensor(dft_w16[:, r, 1], t, dft_w16[:, r, 0], ALU.subtract).then_inc(split_ready, 1)
            stats(0, 1, 0, 28, early=True)
            reciprocal(0, 0)
            stats(0, 1, 28, 40, early=True)
            dve.wait_ge(scale_ready, 1)
            for b in range(FIRST_A, FIRST_D):
                v = x1[0][:, :, b]
                ins = nc.vector.tensor_scalar(v, v, rstd[:, 0, b:b + 1], nbias[:, 0, b:b + 1], ALU.mult, ALU.add)
            ins.then_inc(norm_first, 1)
            stats(0, 1, 40, 2 * B, early=True)
            ends = [0] + [AHEAD * (j + 1) // 3 for j in range(XS - 1)]
            for j in range(XS):
                turn(0, j, EARLY_ROOTS[j], begin=ends[j - 1] if j else 0, end=ends[j])
            with dve.Fori(1, ITER1 - 1) as i:
                for j in range(XS):
                    turn(i, j)
            for j in range(XS):
                turn(ITER1 - 1, j, left=XS - j)

            def build(i, m):
                s, k = m // 2, 2 * (m % 2)
                if m % 2 == 0:
                    dve.wait_ge(pl_loaded[s], (i + 1) * 64 + (0 if s else FIRST_PARTS))
                wait(dve, mix_done, (i * BODY2 + m - 1) * GPQ)
                a = planes[0:C, 2, :, k:k + 2]
                b = planes[C:P, s, :, k:k + 2]
                ins = nc.vector.tensor_copy(a, b)
                if s == 0:
                    ins = nc.vector.tensor_scalar(b, b, -1.0, None, ALU.mult)
                ins.then_inc(pl_dve, 1)

            def build_first():
                dve.wait_ge(pl_loaded[0], 64 + FIRST_PARTS)
                for k, done in enumerate((first_kx, pl_dve)):
                    nc.vector.tensor_copy(planes[0:C, 2, :, k], planes[C:P, 0, :, k])
                    nc.vector.tensor_scalar(planes[C:P, 0, :, k], planes[C:P, 0, :, k], -1.0, None, ALU.mult)\
                        .then_inc(done, 1)

            def keep_max(i):
                dve.wait_ge(w_seen, i * BODY2 * WP)
                dve.wait_ge(w_run_ready, i)
                nc.vector.tensor_tensor(w_run, w_run, w_max, ALU.max).then_inc(w_run_ready, 1)

            def copy_groups(i, m, first=False):
                wait(dve, g_stored[m % 2], i * 64 + (m // 2) * 32)
                for n in range(0, GPQ, 2):
                    k, y = n // (GPQ // 2), n % (GPQ // 2) * GK
                    dve.wait_ge(mix_done, (i * BODY2 + m) * GPQ + n + 1)
                    src = ps_g[(m * GPQ + n) % 4][C * k:C * k + C, 0:GK]
                    dst = g_st[C * k:C * k + C, m % 2, :, y:y + GK].rearrange("p n y -> p y n")
                    nc.vector.tensor_copy(dst, src).then_inc(g_dve, 1)
                    if first and m == 0 and n == 0:
                        build(i, 1)
                    if not (first and m < 2) and n // 2 < WP:
                        weight_max(i, m, n // 2)

            def mix_turn(i, m, first=False, last=False):
                if not last and not (first and m == 0):
                    build(*((i, m + 1) if m + 1 < BODY2 else (i + 1, 0)))
                copy_groups(i, m, first)

            dve.wait_ge(bias_loaded, 16)
            nc.vector.tensor_scalar(bias_w, bias_col, float(W), None, ALU.mult).then_inc(bias_ready, 1)
            build_first()
            for m in range(BODY2):
                mix_turn(0, m, first=True)
                if m == 0:
                    dve.wait_ge(g_dve, 1)
                    dve.wait_ge(bias_ready, 1)
                    dc = g_st[0:CO, 0, 0:B, 0]
                    nc.vector.tensor_scalar(dc, dc, bias_w[0:CO], None, ALU.add).then_inc(bias_added, 1)
            with dve.Fori(1, ITER2 - 1) as i:
                keep_max(i)
                for m in range(BODY2):
                    mix_turn(i, m)
            keep_max(ITER2 - 1)
            for m in range(BODY2):
                mix_turn(ITER2 - 1, m, last=m == BODY2 - 1)
            keep_max(ITER2)

            nc.vector.tensor_copy(inv_w16[:, 0], inv_w).then_inc(split_ready, 1)
            dve.wait_ge(split_ready, 5)
            nc.vector.tensor_tensor(inv_w16[:, 1], inv_w, inv_w16[:, 0], ALU.subtract).then_inc(split_ready, 1)
            dve.wait_ge(w_run_ready, ITER2 + 1)
            nc.vector.tensor_reduce(own_max[:, 0:1], w_run, mybir.AxisListType.X, ALU.max).then_inc(own_max_ready, 1)
            nc.vector.tensor_reduce(own_max[:, 1:2], bias_col, mybir.AxisListType.X, ALU.max,
                                    apply_absolute_value=True).then_inc(own_max_ready, 1)
            dve.wait_ge(all_max_ready, 1)
            nc.vector.tensor_scalar(bound, all_max[:, 1:2], V_PER_BIAS, TINY, ALU.mult, ALU.add)\
                .then_inc(scale_step, 1)
            dve.wait_ge(scale_step, 1)
            nc.vector.scalar_tensor_tensor(out=bound_rec, in0=all_max[:, 0:1], scalar=V_PER_W, in1=bound,
                                           op0=ALU.mult, op1=ALU.add).then_inc(scale_step, 1)
            dve.wait_ge(scale_step, 2)
            nc.vector.tensor_scalar(v_unscale, bound_rec, 1.0 / (V_TOP * W_SCALE * W), None, ALU.mult)\
                .then_inc(scale_step, 1)
            nc.vector.reciprocal(bound, bound_rec).then_inc(scale_step, 1)
            dve.wait_ge(scale_step, 4)
            nc.vector.tensor_scalar(v_scale, bound, V_TOP, None, ALU.mult).then_inc(scale_step, 1)
            dve.wait_ge(scale_step, 5)

            def low_v(i, n):
                dve.wait_ge(v_high, i * BODY3 + n + 1)
                nc.vector.scalar_tensor_tensor(out=v16[:, n % 2, 1], in0=ps_v[n % 2], scalar=v_scale,
                                               in1=v16[:, n % 2, 0], op0=ALU.mult, op1=ALU.subtract)\
                    .then_inc(v_low, 1)

            def add_x(i, n):
                j, b0 = n // UC3, n % UC3 * CH
                if n % UC3 == 0:
                    dve.wait_ge(x3_loaded[j], (i + 1) * 16 * UC3)
                dve.wait_ge(o_done, i * BODY3 + n + 1)
                v = x3[:, j, b0:b0 + CH]
                nc.vector.scalar_tensor_tensor(out=v, in0=ps_o[n % 2], scalar=v_unscale, in1=v,
                                               op0=ALU.mult, op1=ALU.add).then_inc(o_added, 1)

            def out_body(i, first):
                for n in range(BODY3):
                    low_v(i, n)
                    if n:
                        add_x(i, n - 1)
                    elif not first:
                        add_x(i - 1, BODY3 - 1)

            out_body(0, True)
            with dve.Fori(1, ITER3) as i:
                out_body(i, False)
            add_x(ITER3 - 1, BODY3 - 1)

        @block.scalar
        def _(act):
            def root(i, j):
                act.wait_ge(var_ready, i * XS + j + 1)
                nc.scalar.activation(sd[:, j % 2], var[:, j % 2], ACT.Sqrt).then_inc(sd_ready, 1)

            def normalise(i, j, lo, hi):
                if lo == 0:
                    act.wait_ge(scale_ready, i * XS + j + 1)
                for b in range(lo, hi):
                    v = x1[j][:, :, b]
                    ins = nc.scalar.activation(v, v, ACT.Identity, bias=nbias[:, j % 2, b:b + 1],
                                               scale=rstd[:, j % 2, b:b + 1])
                if hi in (NA, FIRST_A):
                    ins.then_inc(norm_act, 1)

            def high_part(i, hh):
                act.wait_ge(t_done, i * BODY1 * 2 + hh + 1)
                m, h = hh // 2, hh % 2
                if h == 0:
                    wait(act, f_done, i * BODY1 + m + 1 - TS)
                dst = t16[:, m % TS, 0, :, :, h * TH:h * TH + TH].rearrange("p r k b -> p b r k")
                nc.scalar.activation(dst, ps_t[hh % TS], ACT.Copy).then_inc(t_high, 1)

            def copy_f(i, m):
                j, n = m // UC, m % UC
                if n == 0:
                    wait(act, f_stored[j % 2], (i * (XS // 2) + j // 2) * 64)
                act.wait_ge(f_done, i * BODY1 + m + 1)
                c, b0 = n // (UC // 2), n % (UC // 2) * CH
                src = ps_f[m % 2].rearrange("p (k b) -> p k b", b=CH)
                nc.scalar.activation(f_sb[:, j % 2, c, :, b0:b0 + CH], src, ACT.Copy,
                                     scale=1.0 / (T_SCALE * W_SCALE)).then_inc(f_copied, 1)

            def copy_z(i):
                act.wait_ge(z_done, i + 1)
                wait(act, z_stored, i * 16)
                nc.scalar.activation(zo_sb, ps_z, ACT.Copy).then_inc(z_copied, 1)

            F_LAG = 3

            def normalised(n, root_at):
                parts = min(UC - 1 - root_at, UC - 2)
                return NA * min(max(n - 1 - root_at, 0), parts) // parts

            def turn(i, j, root_at=0, first=False, left=XS):
                nxt = (i, j + 1) if j + 1 < XS else (i + 1, 0)
                for n in range(UC):
                    m = j * UC + n
                    if left > 1 and n == root_at:
                        root(*nxt)
                    high_part(i, 2 * m)
                    high_part(i, 2 * m + 1)
                    lo, hi = normalised(n, root_at), normalised(n + 1, root_at)
                    if left > 1 and hi > lo:
                        normalise(*nxt, lo, hi)
                    if m >= F_LAG:
                        copy_f(i, m - F_LAG)
                    elif not first:
                        copy_f(i - 1, BODY1 + m - F_LAG)
                    if m == BODY1 - 1:
                        copy_z(i)

            root(0, 0)
            normalise(0, 0, 0, FIRST_A)
            for j in range(XS):
                turn(0, j, EARLY_ROOTS[j], first=True)
            with act.Fori(1, ITER1 - 1) as i:
                for j in range(XS):
                    turn(i, j)
            for j in range(XS):
                turn(ITER1 - 1, j, left=XS - j)
            for m in range(BODY1 - F_LAG, BODY1):
                copy_f(ITER1 - 1, m)

            def build(i, m):
                s, k = m // 2, 2 * (m % 2)
                if m % 2 == 0:
                    act.wait_ge(pl_loaded[s], (i + 1) * 64 + (0 if s else FIRST_PARTS))
                wait(act, mix_done, (i * BODY2 + m - 1) * GPQ)
                nc.scalar.activation(planes[C:P, 2, :, k:k + 2], planes[0:C, s, :, k:k + 2], ACT.Copy,
                                     scale=-1.0 if s else 1.0).then_inc(pl_act, 1)

            def build_first():
                act.wait_ge(pl_loaded[0], 64 + FIRST_PARTS)
                for k, done in enumerate((first_kx, pl_act)):
                    nc.scalar.activation(planes[C:P, 2, :, k], planes[0:C, 0, :, k], ACT.Copy).then_inc(done, 1)

            def copy_groups(i, m, first=False):
                wait(act, g_stored[m % 2], i * 64 + (m // 2) * 32)
                for n in range(1, GPQ, 2):
                    k, y = n // (GPQ // 2), n % (GPQ // 2) * GK
                    act.wait_ge(mix_done, (i * BODY2 + m) * GPQ + n + 1)
                    src = ps_g[(m * GPQ + n) % 4][C * k:C * k + C, 0:GK]
                    dst = g_st[C * k:C * k + C, m % 2, :, y:y + GK].rearrange("p n y -> p y n")
                    nc.scalar.activation(dst, src, ACT.Copy).then_inc(g_act, 1)
                    if first and m == 0 and n == 1:
                        build(i, 1)

            def mix_turn(i, m, first=False, last=False):
                if not last and not (first and m == 0):
                    build(*((i, m + 1) if m + 1 < BODY2 else (i + 1, 0)))
                copy_groups(i, m, first)

            build_first()
            for m in range(BODY2):
                mix_turn(0, m, first=True)
            with act.Fori(1, ITER2 - 1) as i:
                for m in range(BODY2):
                    mix_turn(i, m)
            for m in range(BODY2):
                mix_turn(ITER2 - 1, m, last=m == BODY2 - 1)

            def high_v(i, n):
                act.wait_ge(v_done, i * BODY3 + n + 1)
                wait(act, o_done, i * BODY3 + n - 1)
                nc.scalar.activation(v16[:, n % 2, 0], ps_v[n % 2], ACT.Copy, scale=v_scale).then_inc(v_high, 1)

            act.wait_ge(scale_step, 5)
            for n in range(BODY3):
                high_v(0, n)
            with act.Fori(1, ITER3) as i:
                for n in range(BODY3):
                    high_v(i, n)

        @block.tensor
        def _(pe):
            def dft_rows(i, m):
                j, n = m // UC, m % UC
                if n == 0:
                    pe.wait_ge(norm_pool, i * XS + j + 1)
                    pe.wait_ge(norm_act, i * XS + j + 1)
                c, b0 = n // (UC // 2), n % (UC // 2) * CH
                for h in range(2):
                    wait(pe, t_low, (i * BODY1 + m) * 2 + h + 1 - TS)
                    for b in range(TH):
                        ins = nc.tensor.matmul(ps_t[(2 * m + h) % TS][:, b].rearrange("p r k -> p (r k)"),
                                               x1[j][:, c, b0 + h * TH + b], dft_h, start=True, stop=True)
                    ins.then_inc(t_done, 1)

            def dft_cols(i, m):
                pe.wait_ge(t_low, (i * BODY1 + m) * 2 + 2)
                wait(pe, f_copied, i * BODY1 + m - 1)
                terms = [(r, a, b) for r in range(2) for a, b in ((0, 0), (1, 0), (0, 1))]
                for n, (r, a, b) in enumerate(terms):
                    ins = nc.tensor.matmul(ps_f[m % 2], dft_w16[:, r, a],
                                           t16[:, m % TS, b, r].rearrange("p k b -> p (k b)"),
                                           start=(n == 0), stop=(n == len(terms) - 1))
                ins.then_inc(f_done, 1)

            def dft_nyquist(i):
                pe.wait_ge(z_ready, (i + 1) * XS)
                wait(pe, z_copied, i)
                nc.tensor.matmul(ps_z, dft_z, z_sb.rearrange("p a c b -> p (a c b)"),
                                 start=True, stop=True).then_inc(z_done, 1)

            LAG = 2

            def body(i, first):
                for m in range(BODY1):
                    if m == (XS - 1) * UC + 1:
                        dft_nyquist(i)
                    dft_rows(i, m)
                    if m >= LAG:
                        dft_cols(i, m - LAG)
                    elif not first:
                        dft_cols(i - 1, BODY1 + m - LAG)

            pe.wait_ge(tab_loaded, 16)
            pe.wait_ge(split_ready, 4)
            pe.wait_ge(norm_first, 1)
            body(0, True)
            with pe.Fori(1, ITER1) as i:
                body(i, False)
            for m in range(BODY1 - LAG, BODY1):
                dft_cols(ITER1 - 1, m)

            pe.wait_ge(f_copied, ITER1 * BODY1)
            pe.wait_ge(z_copied, ITER1)

            def mix_pair(i, m, first=False):
                s = m // 2
                pe.wait_ge(w_loaded[m % 2], i * 64 + (m // 2 + 1) * 32)
                if first and m == 0:
                    pe.wait_ge(first_kx, 2)
                for n in range(GPQ):
                    if n == (GPQ // 2 if first and m == 0 else 0):
                        pe.wait_ge(pl_dve, i * BODY2 + m + 1)
                        pe.wait_ge(pl_act, i * BODY2 + m + 1)
                    seen = (m * GPQ + n) // 2 - 1
                    wait(pe, g_dve if n % 2 == 0 else g_act, i * (BODY2 * GPQ // 2) + seen)
                    k, y0 = n // (GPQ // 2), n % (GPQ // 2) * GK
                    if n == GPQ - 1:
                        pe.wait_ge(w_seen, (i * BODY2 + m + 1) * WP)
                    for y in range(GK):
                        ins = nc.tensor.matmul(ps_g[(m * GPQ + n) % 4][C * k:C * k + C, y],
                                               w_sb[:, m % 2, :, k * KY + y0 + y],
                                               planes[:, s::2 - s, y0 + y, 2 * (m % 2) + k, :],
                                               start=True, stop=True)
                    ins.then_inc(mix_done, 1)

            for m in range(BODY2):
                mix_pair(0, m, first=True)
            with pe.Fori(1, ITER2) as i:
                for m in range(BODY2):
                    mix_pair(i, m)

            pe.wait_ge(split_ready, 6)
            pe.wait_ge(g_dve, NQ * GPQ // 2)
            pe.wait_ge(g_act, NQ * GPQ // 2)

            def inverse_rows(i, n):
                j, b0 = n // UC3, n % UC3 * CH
                if n % UC3 == 0:
                    pe.wait_ge(g3_loaded[j], i * 16 + 16)
                wait(pe, v_low, i * BODY3 + n - 1)
                for c in range(CH):
                    for r, t in enumerate((inv_r, inv_i)):
                        ins = nc.tensor.matmul(ps_v[n % 2][KH * r:KH * r + KH, c], g3[:, j, b0 + c, r:r + KH], t,
                                               start=True, stop=True)
                ins.then_inc(v_done, 1)

            def inverse_cols(i, n):
                pe.wait_ge(v_low, i * BODY3 + n + 1)
                wait(pe, o_added, i * BODY3 + n - 1)
                for c in range(CH):
                    for t, (a, b) in enumerate(((0, 0), (0, 1), (1, 0))):
                        ins = nc.tensor.matmul(ps_o[n % 2][:, c], v16[:, n % 2, a, c], inv_w16[:, b],
                                               start=(t == 0), stop=(t == 2))
                ins.then_inc(o_done, 1)

            def inverse_body(i, first):
                for n in range(BODY3):
                    inverse_rows(i, n)
                    if n:
                        inverse_cols(i, n - 1)
                    elif not first:
                        inverse_cols(i - 1, BODY3 - 1)

            inverse_body(0, True)
            with pe.Fori(1, ITER3) as i:
                inverse_body(i, False)
            inverse_cols(ITER3 - 1, BODY3 - 1)


def dft_tables(n, kx, ky):
    import numpy as np

    a = 2 * np.pi / n
    p = np.arange(n)[:, None]
    k = np.arange(kx)[None, :]
    c, s = np.cos(a * p * k), np.sin(a * p * k)
    dft_h = np.concatenate([c, -s], 1) / n * 2048
    dft_wr = np.concatenate([c, -s], 1) * 256
    dft_wi = np.concatenate([s, c], 1) * 256
    dft_z = np.concatenate([s, c], 1) / n * (n // 2)
    h = np.arange(n)[None, :]
    kk = np.arange(kx)[:, None]
    c, s = np.cos(a * kk * h), np.sin(a * kk * h)
    odd = (kk // 4 % 2 == 1)[:, :, None]
    inv_r, inv_i = (np.where(odd, t[:, ::-1], t).reshape(2 * kx, n) for t in (np.stack([c, -s], 1), np.stack([s, c], 1)))
    y = np.arange(ky)[:, None]
    cy, sy = np.cos(a * y * h), np.sin(a * y * h)
    weight = np.where((y == 0) | (y == ky - 1), 1.0, 2.0) * 256
    inv_w = np.concatenate([(weight * cy)[:ky - 1], (-weight * sy)[1:ky - 1], (weight * cy)[ky - 1:]], 0)
    return np.ascontiguousarray(np.concatenate([dft_h, dft_wr, dft_wi, dft_z, inv_r, inv_i, inv_w], 1), np.float32)


_INS = ["x", "L0_conv_weights_real", "L0_conv_weights_imag", "L0_conv_bias"]


def kernel(**inputs):
    import numpy as _np
    import concourse.bacc as _bacc
    from concourse import mybir as _mybir
    from concourse.bass_utils import run_bass_kernel_spmd as _run

    nc = _bacc.Bacc("TRN2", target_bir_lowering=False, num_devices=1)
    arrays, args = {}, []
    for name in _INS:
        arrays[f"in_{name}_dram"] = _np.ascontiguousarray(inputs[name])
    n = inputs["x"].shape[-1]
    arrays["in_tables_dram"] = dft_tables(n, n // 2, n // 2 + 1)
    for name, a in arrays.items():
        args.append(nc.dram_tensor(name, a.shape, _mybir.dt.from_np(a.dtype), kind="ExternalInput").ap())
    shape = tuple(inputs["x"].shape)
    args.append(nc.dram_tensor("out_0_dram", shape, _mybir.dt.float32, kind="ExternalOutput").ap())
    spectral_conv_kernel(nc, *args)
    r = _run(nc, [arrays], core_ids=[0])
    return r.results[0]["out_0_dram"]
```
